# Optimizing a Trainium2 kernel written in Bass

```python
import numpy as np
import jax
import jax.numpy as jnp

def _softmax(x, axis=-1):
    return jax.nn.softmax(x, axis=axis)

def _gelu(x):
    return jax.nn.gelu(x, approximate=True)

def _silu(x):
    return jax.nn.silu(x)

def _sigmoid(x):
    return jax.nn.sigmoid(x)

def _layernorm(x, axis=-1, eps=1e-05):
    m = jnp.mean(x, axis=axis, keepdims=True)
    v = jnp.var(x, axis=axis, keepdims=True)
    return (x - m) / jnp.sqrt(v + eps)

def _scatter_add(tgt, idx, src, axis=0):
    return tgt.at[idx].add(src)

def _segment_sum(src, seg, n):
    return jax.ops.segment_sum(src, seg, n)
kernel_name = 'mk_xattn_ffn_d2_seqx_r4_faa24a'

def setup_inputs(seed: int=0):
    np.random.seed(seed)
    _w = jnp.asarray

    def _rec_inputs():
        import jax
        import jax.numpy as jnp
        _rk = jax.random.key(seed)
        x = -7.109e-05 + 0.9999 * jax.random.normal(jax.random.fold_in(_rk, 1), (4, 512, 512), jnp.float32)
        _lenS = 512 - jax.random.randint(jax.random.fold_in(_rk, 7), (4,), 0, max(1, 512 // 4) + 1, jnp.int32)
        _lenS2 = 512 - jax.random.randint(jax.random.fold_in(_rk, 8), (4,), 0, max(1, 512 // 4) + 1, jnp.int32)
        _ctx_512P = jax.random.normal(jax.random.fold_in(_rk, 11), (4, 16, 128), jnp.float32)
        _ctx_512c = jax.random.dirichlet(jax.random.fold_in(_rk, 511), 0.3 * jnp.ones((16,), jnp.float32), (4, 512))
        _ctx_512t = jnp.einsum('bsk,bkd->bsd', _ctx_512c, _ctx_512P)
        _ctx_512t = _ctx_512t * jax.lax.rsqrt(jnp.mean(jnp.square(_ctx_512t)) + 1e-12) * 0.953939
        ctx_512 = 2.81802e-05 + 1.00001 * (_ctx_512t + 0.3 * jax.random.normal(jax.random.fold_in(_rk, 611), (4, 512, 128), jnp.float32))
        return (x, ctx_512)
    x, ctx_512 = _rec_inputs()

    def _L0_xattn_setup():
        import jax, jax.numpy as jnp
        import numpy as np
        EPS = 1e-06
        IMAGE_DIMS = 512
        key = jax.random.key(seed)
        k1, k2, k3 = jax.random.split(key, 3)
        B, I, J, D = (16, 512, 512, 128)
        p = jax.random.normal(k1, (B, I, J), dtype=jnp.float32)
        k_v = jax.random.normal(k2, (B, J, D), dtype=jnp.float32)
        W_k = jax.random.normal(k3, (D, D), dtype=jnp.float32) * (1.0 / np.sqrt(D))
        b_k = jnp.zeros((D,), dtype=jnp.float32)
        ln_gamma = jnp.ones((J,), dtype=jnp.float32)
        ln_beta = jnp.zeros((J,), dtype=jnp.float32)
        return {'p': p, 'k_v': k_v, 'W_k': W_k, 'b_k': b_k, 'ln_gamma': ln_gamma, 'ln_beta': ln_beta}
    _L0_xattn_all = _L0_xattn_setup()
    _L0_xattn_in = {k: v for k, v in _L0_xattn_all.items() if k in ('W_k', 'b_k', 'ln_gamma', 'ln_beta')}
    del _L0_xattn_all

    def _L0_ffn_setup():
        import jax, jax.numpy as jnp
        import numpy as np
        TOP_K = 4
        ROUTED_SCALE = 1.0
        NORM_TOPK = True
        B, S, H = (1, 512, 512)
        E, I = (16, 192)
        IS = 192
        key = jax.random.key(seed)
        ks = jax.random.split(key, 8)
        s = 0.02
        return {'hidden_states': jax.random.normal(ks[0], (B, S, H), jnp.float32), 'router_w': jax.random.normal(ks[1], (E, H), jnp.float32) * s, 'e_bias': jax.random.normal(ks[2], (E,), jnp.float32) * s, 'gate_up_proj': jax.random.normal(ks[3], (E, 2 * I, H), jnp.float32) * s, 'down_proj': jax.random.normal(ks[4], (E, H, I), jnp.float32) * s, 'shared_gate_w': jax.random.normal(ks[5], (IS, H), jnp.float32) * s, 'shared_up_w': jax.random.normal(ks[6], (IS, H), jnp.float32) * s, 'shared_down_w': jax.random.normal(ks[7], (H, IS), jnp.float32) * s}
    _L0_ffn_all = _L0_ffn_setup()
    _L0_ffn_in = {k: v for k, v in _L0_ffn_all.items() if k in ('router_w', 'e_bias', 'gate_up_proj', 'down_proj', 'shared_gate_w', 'shared_up_w', 'shared_down_w')}
    del _L0_ffn_all

    def _L1_xattn_setup():
        import jax, jax.numpy as jnp
        import numpy as np
        B, S, H, NH, L = (2, 512, 512, 16, 128)
        HD = H // NH
        key = jax.random.key(seed)
        k1, k2, k3, k4, k5 = jax.random.split(key, 5)
        scale = 0.02
        return {'q': jax.random.normal(k1, (B, S, H), dtype=jnp.float32), 'latent_kv': jax.random.normal(k2, (B, S, L), dtype=jnp.float32), 'Wq': jax.random.normal(k3, (H, H), dtype=jnp.float32) * scale, 'Wkv_expand': jax.random.normal(k4, (2 * H, L), dtype=jnp.float32) * scale, 'Wout': jax.random.normal(k5, (H, H), dtype=jnp.float32) * scale}
    _L1_xattn_all = _L1_xattn_setup()
    _L1_xattn_in = {k: v for k, v in _L1_xattn_all.items() if k in ('Wq', 'Wkv_expand', 'Wout')}
    del _L1_xattn_all

    def _L1_ffn_setup():
        import jax, jax.numpy as jnp
        import numpy as np
        D_MODEL = 512
        D_FF = 2048
        BATCH = 4
        SEQ = 512
        MAX_EXP = 4
        NUM_BITS = 8
        C_CHUNKS = 2
        SCALE = 0.1

        def _pow2_ternary(key, out_dim, in_dim, max_exp):
            k1, k2 = jax.random.split(key)
            t = jax.random.randint(k1, (out_dim, in_dim), -1, 2).astype(jnp.float32)
            e = jax.random.randint(k2, (out_dim, in_dim), 0, max_exp + 1).astype(jnp.float32)
            return t * jnp.exp2(-e)

        def _lookup_act(h):
            total_bits = NUM_BITS * C_CHUNKS
            qmax = 2 ** (total_bits - 1) - 1
            qmin = -2 ** (total_bits - 1)
            q = jnp.clip(jnp.round(h / SCALE), qmin, qmax)
            return jax.nn.gelu(q * SCALE)
        key = jax.random.key(seed)
        kx, k1, k2 = jax.random.split(key, 3)
        x = jax.random.normal(kx, (BATCH, SEQ, D_MODEL), dtype=jnp.float32)
        W1 = _pow2_ternary(k1, D_FF, D_MODEL, MAX_EXP)
        W2 = _pow2_ternary(k2, D_MODEL, D_FF, MAX_EXP)
        return {'x': x, 'W1': W1, 'W2': W2}
    _L1_ffn_all = _L1_ffn_setup()
    _L1_ffn_in = {k: v for k, v in _L1_ffn_all.items() if k in ('W1', 'W2')}
    del _L1_ffn_all
    return {'x': x, 'ctx_512': ctx_512, 'L0_xattn_W_k': _L0_xattn_in['W_k'], 'L0_xattn_b_k': _L0_xattn_in['b_k'], 'L0_xattn_ln_gamma': _L0_xattn_in['ln_gamma'], 'L0_xattn_ln_beta': _L0_xattn_in['ln_beta'], 'L0_ffn_router_w': _L0_ffn_in['router_w'], 'L0_ffn_e_bias': _L0_ffn_in['e_bias'], 'L0_ffn_gate_up_proj': _L0_ffn_in['gate_up_proj'], 'L0_ffn_down_proj': _L0_ffn_in['down_proj'], 'L0_ffn_shared_gate_w': _L0_ffn_in['shared_gate_w'], 'L0_ffn_shared_up_w': _L0_ffn_in['shared_up_w'], 'L0_ffn_shared_down_w': _L0_ffn_in['shared_down_w'], 'L1_xattn_Wq': _L1_xattn_in['Wq'], 'L1_xattn_Wkv_expand': _L1_xattn_in['Wkv_expand'], 'L1_xattn_Wout': _L1_xattn_in['Wout'], 'L1_ffn_W1': _L1_ffn_in['W1'], 'L1_ffn_W2': _L1_ffn_in['W2']}

def reference(x, ctx_512, L0_xattn_W_k, L0_xattn_b_k, L0_xattn_ln_gamma, L0_xattn_ln_beta, L0_ffn_router_w, L0_ffn_e_bias, L0_ffn_gate_up_proj, L0_ffn_down_proj, L0_ffn_shared_gate_w, L0_ffn_shared_up_w, L0_ffn_shared_down_w, L1_xattn_Wq, L1_xattn_Wkv_expand, L1_xattn_Wout, L1_ffn_W1, L1_ffn_W2):
    import jax
    import jax.numpy as jnp

    def _L0_xattn_ref(p, k_v, W_k, b_k, ln_gamma, ln_beta):
        import jax, jax.numpy as jnp
        import numpy as np
        EPS = 1e-06
        IMAGE_DIMS = 512
        kv = k_v @ W_k.T + b_k
        out = jnp.einsum('bij,bjd->bid', p, kv)
        scale = IMAGE_DIMS ** (-0.5)
        sim = jnp.einsum('bid,bjd->bij', out, kv) * scale
        mu = jnp.mean(sim, axis=-1, keepdims=True)
        var = jnp.var(sim, axis=-1, keepdims=True)
        sim = (sim - mu) * jax.lax.rsqrt(var + EPS) * ln_gamma + ln_beta
        attn = jax.nn.softmax(sim, axis=-1)
        return attn

    def _L0_ffn_ref(hidden_states, router_w, e_bias, gate_up_proj, down_proj, shared_gate_w, shared_up_w, shared_down_w):
        import jax, jax.numpy as jnp
        import numpy as np
        TOP_K = 4
        ROUTED_SCALE = 1.0
        NORM_TOPK = True
        B, S, H = (1, 512, 512)
        E, I = (16, 192)
        IS = 192
        orig_shape = hidden_states.shape
        x = hidden_states.reshape(-1, orig_shape[-1])
        T = x.shape[0]
        scores = jax.nn.sigmoid(x @ router_w.T)
        _, topk_idx = jax.lax.top_k(scores + e_bias[None, :], TOP_K)
        topk_w = jnp.take_along_axis(scores, topk_idx, axis=1)
        if NORM_TOPK:
            topk_w = topk_w / (topk_w.sum(axis=-1, keepdims=True) + 1e-20)
        topk_w = topk_w * ROUTED_SCALE
        combine = jnp.zeros((T, E), x.dtype).at[jnp.arange(T)[:, None], topk_idx].add(topk_w)

        def step(acc, xs):
            gu_w, d_w, c = xs
            gu = x @ gu_w.T
            g, u = jnp.split(gu, 2, axis=1)
            y = jax.nn.silu(g) * u @ d_w.T
            return (acc + c[:, None] * y, None)
        routed, _ = jax.lax.scan(step, jnp.zeros_like(x), (gate_up_proj, down_proj, combine.T))
        shared = jax.nn.silu(x @ shared_gate_w.T) * (x @ shared_up_w.T) @ shared_down_w.T
        return (routed + shared).reshape(orig_shape)

    def _L1_xattn_ref(q, latent_kv, Wq, Wkv_expand, Wout):
        import jax, jax.numpy as jnp
        import numpy as np
        B, S, H, NH, L = (2, 512, 512, 16, 128)
        HD = H // NH
        b, sq, _ = q.shape
        sk = latent_kv.shape[1]
        qp = q @ Wq.T
        kv = latent_kv @ Wkv_expand.T
        k, v = jnp.split(kv, 2, axis=-1)
        qh = qp.reshape(b, sq, NH, HD).transpose(0, 2, 1, 3)
        kh = k.reshape(b, sk, NH, HD).transpose(0, 2, 1, 3)
        vh = v.reshape(b, sk, NH, HD).transpose(0, 2, 1, 3)
        inv_sqrt_d = 1.0 / jnp.sqrt(jnp.float32(HD))
        scores = jnp.einsum('bhqd,bhkd->bhqk', qh, kh) * inv_sqrt_d
        causal = jnp.tril(jnp.ones((sq, sk), dtype=bool))
        scores = jnp.where(causal, scores, jnp.finfo(scores.dtype).min)
        attn = jax.nn.softmax(scores, axis=-1)
        out = jnp.einsum('bhqk,bhkd->bhqd', attn, vh)
        out = out.transpose(0, 2, 1, 3).reshape(b, sq, H)
        return out @ Wout.T

    def _L1_ffn_ref(x, W1, W2):
        import jax, jax.numpy as jnp
        import numpy as np
        D_MODEL = 512
        D_FF = 2048
        BATCH = 4
        SEQ = 512
        MAX_EXP = 4
        NUM_BITS = 8
        C_CHUNKS = 2
        SCALE = 0.1

        def _pow2_ternary(key, out_dim, in_dim, max_exp):
            k1, k2 = jax.random.split(key)
            t = jax.random.randint(k1, (out_dim, in_dim), -1, 2).astype(jnp.float32)
            e = jax.random.randint(k2, (out_dim, in_dim), 0, max_exp + 1).astype(jnp.float32)
            return t * jnp.exp2(-e)

        def _lookup_act(h):
            total_bits = NUM_BITS * C_CHUNKS
            qmax = 2 ** (total_bits - 1) - 1
            qmin = -2 ** (total_bits - 1)
            q = jnp.clip(jnp.round(h / SCALE), qmin, qmax)
            return jax.nn.gelu(q * SCALE)
        h = jnp.einsum('bsd,fd->bsf', x, W1)
        a = _lookup_act(h)
        return jnp.einsum('bsf,df->bsd', a, W2)
    x = x + _L0_xattn_ref(_layernorm(x, axis=-1), ctx_512, L0_xattn_W_k, L0_xattn_b_k, L0_xattn_ln_gamma, L0_xattn_ln_beta)
    x = x + _L0_ffn_ref(_layernorm(x, axis=-1), L0_ffn_router_w, L0_ffn_e_bias, L0_ffn_gate_up_proj, L0_ffn_down_proj, L0_ffn_shared_gate_w, L0_ffn_shared_up_w, L0_ffn_shared_down_w)
    x = x + _L1_xattn_ref(_layernorm(x, axis=-1), ctx_512, L1_xattn_Wq, L1_xattn_Wkv_expand, L1_xattn_Wout)
    x = x + _L1_ffn_ref(_layernorm(x, axis=-1), L1_ffn_W1, L1_ffn_W2)
    return x

_drawn_inputs = setup_inputs


def setup_inputs(seed=0):
    import zlib

    import numpy as np

    out = dict(_drawn_inputs(seed))
    spreads = {'L0_xattn_b_k': (0.0, 2.0),
     'L0_xattn_ln_gamma': (1.0, 0.6),
     'L0_xattn_ln_beta': (0.0, 0.8)}
    factors = {'L0_xattn_W_k': 8.0,
     'L0_ffn_router_w': 4.18,
     'L0_ffn_e_bias': 8.0,
     'L0_ffn_gate_up_proj': 3.629,
     'L0_ffn_down_proj': 3.64,
     'L1_xattn_Wq': 31.809}
    for name, (base, spread) in spreads.items():
        noise = np.random.default_rng([zlib.crc32(name.encode()), seed]).standard_normal(out[name].shape)
        drawn = base * np.exp(spread * noise) if base else spread * noise
        out[name] = jnp.asarray(drawn.astype(out[name].dtype))
    for name, factor in factors.items():
        out[name] = (out[name] * factor).astype(out[name].dtype)
    return out
```

```python
from contextlib import ExitStack

import numpy as np

import concourse.bass as bass
from concourse import mybir

ACT = mybir.ActivationFunctionType
ALU = mybir.AluOpType
F32 = mybir.dt.float32
F16 = mybir.dt.float16
I16 = mybir.dt.int16
I32 = mybir.dt.int32
U32 = mybir.dt.uint32
AX = mybir.AxisListType

P = 128
B, S, H = 4, 512, 512
T = B * S
NT = T // P
TB = S // P
KC = H // P
CD = 128
E, TOPK, EI = 16, 4, 192
FF = 2048
NH, HD = 16, 32
HG = P // HD
NG = NH // HG

QT = T * TOPK // P + E
XS, WS, HS, QS = 2048.0, 256.0, 16.0, 16.0
LN_EPS, SIM_EPS = 1e-5, 1e-6
BIG = 3.0e38

GU = 2 * EI
W_GU_HI, W_GU_LO = 0, KC * GU
W_D0_HI, W_D0_LO = 2 * KC * GU, 2 * KC * GU + H
W_D1 = W_D0_LO + H
EW = W_D1 + H
EWF = KC * GU + 2 * H


class Scope:

    def __init__(self, nc, stage):
        self.nc, self.stage, self.stack, self.made = nc, stage, ExitStack(), []

    def __enter__(self):
        return self

    def __exit__(self, *e):
        if self.made and e[0] is None:
            with self.nc.Block() as block:
                @block.sync
                def _(sp):
                    for sem in self.made:
                        sp.sem_clear(sem)
        return self.stack.__exit__(*e)

    def sb(self, name, shape, dt=F32):
        return self.stack.enter_context(self.nc.sbuf_tensor(f"{self.stage}_{name}", shape, dt))

    def ps(self, name, shape, dt=F32):
        return self.stack.enter_context(self.nc.psum_tensor(f"{self.stage}_{name}", shape, dt))

    def sems(self, names):
        made = [self.stack.enter_context(self.nc.semaphore(f"{self.stage}_{n}")) for n in names.split()]
        self.made += made
        return made

    def gpsimd_dma_sems(self, names):
        return [self.nc.alloc_semaphore(f"{self.stage}_{n}") for n in names.split()]

    def block(self):
        return self.nc.Block()


def attention0(nc, d, W, logits, ident):
    with Scope(nc, "a0") as s:
        wk = W[:, E, 8 * H:8 * H + 2 * CD].bitcast(F32)
        bk_col = s.sb("bk_col", [P, 1])
        bk_row = W[:, E, 8 * H + 2 * CD:8 * H + 4 * CD].bitcast(F32)
        gamma = s.sb("gamma", [P, S])
        beta = s.sb("beta", [P, S])
        wr = s.sb("wr", [P, KC, E])
        xt = s.sb("xt", [P, 2, TB, H])
        ctxT = s.sb("ctxT", [P, 2, S])
        kv = s.sb("kv", [P, TB, CD])
        kvT = s.sb("kvT", [P, S])
        p = s.sb("p", [P, TB, H])
        outT = W[:, E, 6 * H:8 * H].bitcast(F32)
        pT = s.sb("pT", [P, KC, S])
        z = pT
        pair = W[:, E, 0:4 * H].rearrange("p (s n) -> p s n", s=2)
        xnT = W[:, E, 4 * H:6 * H].bitcast(F32)
        mhalf = s.sb("mhalf", [P, TB])
        st = s.sb("st", [P, TB, 6])
        mv = s.sb("mv", [P, TB, 2])
        var = s.sb("var", [P, TB])
        rstd = s.sb("rstd", [P, TB])
        st2 = s.sb("st2", [P, TB, 6])
        mv2 = s.sb("mv2", [P, TB, 2])
        var2 = s.sb("var2", [P, TB])
        rstd2 = s.sb("rstd2", [P, TB])
        coef = s.sb("coef", [P, TB])
        nb = s.sb("nb", [P, TB])
        mx = s.sb("mx", [P, TB])
        nmx = s.sb("nmx", [P, TB])
        ssum = s.sb("ssum", [P, TB])
        rsum = s.sb("rsum", [P, TB])
        st3 = s.sb("st3", [P, TB, 6])
        mv3 = s.sb("mv3", [P, TB, 2])
        var3 = s.sb("var3", [P, TB])
        rstd3 = s.sb("rstd3", [P, TB])
        CH = 2 * GU
        stage = s.sb("stage", [P, 2, CH])

        kv_ps = s.ps("kv_ps", [P, TB, CD])
        kvT_ps = s.ps("kvT_ps", [P, S])
        tr_ps = [s.ps(f"tr_ps{i}", [P, KC, P]) for i in range(2)]
        sim_ps = [s.ps(f"sim_ps{i}", [P, S]) for i in range(TB)]

        (consts_in, mhalf_set, kv_done, kvT_done, kv_copied, kvT_copied, ln1_stat, ln1_aggr, ln1_var, ln1_rstd,
         p_ready, pT_done, pT_copied, outT_done, outT_copied, sim_done, s_stat, s_aggr, s_var, s_rstd, s_coef,
         s_nb, z_done, zg_done, zb_done, nmx_done, exp_done, rs_done, x1_done, ln2_stat, ln2_aggr, ln2_var,
         ln2_rstd, xn_done, hi_done, lo_done, xnT_done, xnT_copied, logits_done, logits_copied, w_hi, w_lo) = s.sems(
            "consts_in mhalf_set kv_done kvT_done kv_copied kvT_copied ln1_stat ln1_aggr ln1_var ln1_rstd "
            "p_ready pT_done pT_copied outT_done outT_copied sim_done s_stat s_aggr s_var s_rstd s_coef "
            "s_nb z_done zg_done zb_done nmx_done exp_done rs_done x1_done ln2_stat ln2_aggr ln2_var "
            "ln2_rstd xn_done hi_done lo_done xnT_done xnT_copied logits_done logits_copied w_hi w_lo")
        x_in = s.sems("x_in0 x_in1")
        ctx_in = s.sems("ctx_in0 ctx_in1")
        w_in = s.sems("w_in0 w_in1")
        x1_out = [s.gpsimd_dma_sems(f"x1_out{j}0 x1_out{j}1 x1_out{j}2 x1_out{j}3") for j in range(2)]
        pair_out = s.gpsimd_dma_sems("pair_out0 pair_out1")
        NCONST = 6
        CHUNKS = [(0, CH, W_GU_HI, W_GU_LO), (CH, CH, W_GU_HI + CH, W_GU_LO + CH), (2 * CH, H, W_D0_HI, W_D0_LO),
                  (2 * CH + H, H, W_D1, W_D1)]
        PERB = 4 * len(CHUNKS)

        def chunk_of(b, c):
            return b * 4 + c // 4, CHUNKS[c % 4], c % 2

        with s.block() as block:
            @block.sync
            def _(sp):
                for dst, src in ((wk, d["wkT"]), (bk_col, d["bk_col"]), (gamma, d["gamma"].partition_broadcast(P)),
                                 (beta, d["beta"].partition_broadcast(P)), (bk_row, d["bk"].partition_broadcast(P)),
                                 (wr, d["wr"])):
                    sp.dma_start(dst[:], src).then_inc(consts_in, 16)
                with sp.Fori(0, B // 2) as bb:
                    for j in range(2):
                        b = bb * 2 + j
                        for t in range(TB):
                            sp.wait_ge(x1_out[j][t], bb * 16)
                        sp.dma_start(xt[:, j], d["x"][:, bass.ds(b * TB, TB), :]).then_inc(x_in[j], 16)
                        sp.wait_ge(kv_done, bb * 2)
                        sp.dma_start(ctxT[:, j], d["ctxT"][:, bass.ds(b * S, S)]).then_inc(ctx_in[j], 16)
                        for c in range(PERB):
                            e, (at, n, hi, lo), k = chunk_of(b, c)
                            sp.wait_ge(w_lo, b * PERB + max(c - 1, 0))
                            sp.dma_start(stage[:, k, 0:n], d["wexp"][bass.ds(e, 1), :, at:at + n]
                                         .rearrange("a p n -> p (a n)")).then_inc(w_in[k], 16)

            @block.gpsimd
            def _(pool):
                pool.memset(mhalf[:], -0.5).then_inc(mhalf_set, 1)
                pool.wait_ge(mhalf_set, 1)
                pool.wait_ge(consts_in, 16 * NCONST)
                with pool.Fori(0, B // 2) as bb:
                  for j in range(2):
                    b = bb * 2 + j
                    pool.wait_ge(ln1_var, b + 1)
                    nc.gpsimd.tensor_tensor(rstd[:], var[:], mhalf[:], ALU.pow).then_inc(ln1_rstd, 1)
                    pool.wait_ge(s_var, b + 1)
                    nc.gpsimd.tensor_tensor(rstd2[:], var2[:], mhalf[:], ALU.pow).then_inc(s_rstd, 1)
                    for t in range(TB):
                        pool.wait_ge(z_done, b * TB + t + 1)
                        nc.gpsimd.tensor_tensor(z[:, t], z[:, t], gamma[:], ALU.mult).then_inc(zg_done, 1)
                    pool.wait_ge(ln2_var, b + 1)
                    nc.gpsimd.tensor_tensor(rstd3[:], var3[:], mhalf[:], ALU.pow).then_inc(ln2_rstd, 1)
                    for t in range(TB):
                        pool.wait_ge(lo_done, b * TB + t + 1)
                        pool.dma_start(d["x1"][:, bass.ds(b * TB + t, 1), :], xt[:, j, t:t + 1, :]).then_inc(x1_out[j][t], 16)
                        pool.dma_start(d["pairs"][bass.ds((b * TB + t) * P, P), :], pair[:, t % 2]).then_inc(pair_out[t % 2], 16)
                for q in x1_out[0] + x1_out[1]:
                    pool.wait_ge(q, 16 * B // 2)
                for q in pair_out:
                    pool.wait_ge(q, 16 * B * TB // 2)

            @block.scalar
            def _(act):
                with act.Fori(0, B) as b:
                    def split_hi(c):
                        e, (at, n, hi, lo), k = chunk_of(b, c)
                        act.wait_ge(w_in[k], b * (PERB // 2) * 16 + (c // 2) * 16 + 16)
                        act.activation(W[:, bass.ds(e, 1), hi:hi + n].rearrange("p a n -> p (a n)"),
                                       stage[:, k, 0:n], ACT.Copy, scale=WS).then_inc(w_hi, 1)
                    act.wait_ge(consts_in, 16 * NCONST)
                    act.wait_ge(kvT_done, b + 1)
                    act.wait_ge(sim_done, b * TB)
                    act.activation(kvT[:], kvT_ps[:], ACT.Identity, bias=bk_col[:, 0:1]).then_inc(kvT_copied, 1)
                    for c in range(0, 6):
                        split_hi(c)
                    for t in range(TB):
                        act.wait_ge(pT_done, b * TB + t + 1)
                        if t == 0:
                            act.wait_ge(x1_done, b * TB)
                        act.activation(pT[:, :, t * P:(t + 1) * P], tr_ps[t % 2][:], ACT.Copy).then_inc(pT_copied, 1)
                    act.wait_ge(outT_done, b + 1)
                    act.activation(outT[:], kvT_ps[:], ACT.Copy).then_inc(outT_copied, 1)
                    for c in range(6, 9):
                        split_hi(c)
                    act.wait_ge(s_nb, b + 1)
                    for t in range(TB):
                        act.activation(z[:, t], sim_ps[t][:], ACT.Identity, bias=nb[:, t:t + 1],
                                       scale=coef[:, t:t + 1]).then_inc(z_done, 1)
                    for t in range(TB):
                        act.wait_ge(nmx_done, b * TB + t + 1)
                        act.activation(z[:, t], z[:, t], ACT.Exp, bias=nmx[:, t:t + 1],
                                       accum_out=ssum[:, t:t + 1]).then_inc(exp_done, 1)
                    for c in range(9, PERB):
                        split_hi(c)
                    for t in range(TB):
                        act.wait_ge(xn_done, b * TB + t + 1)
                        if t < 2:
                            act.wait_ge(pair_out[t], b * 32)
                        else:
                            act.wait_ge(pair_out[t - 2], b * 32 + 16)
                        act.activation(pair[:, t % 2, 0:H], p[:, t], ACT.Copy, scale=XS).then_inc(hi_done, 1)
                        act.wait_ge(xnT_done, b * TB + t + 1)
                        act.wait_ge(logits_done, b * TB + t)
                        act.activation(xnT[:], tr_ps[t % 2][:], ACT.Copy).then_inc(xnT_copied, 1)

            @block.tensor
            def _(pe):
                pe.wait_ge(consts_in, 16 * NCONST)
                with pe.Fori(0, B // 2) as bb:
                    for j in range(2):
                        b = bb * 2 + j
                        pe.wait_ge(ctx_in[j], bb * 16 + 16)
                        pe.wait_ge(outT_copied, b)
                        pe.matmul(kvT_ps[:], wk[:], ctxT[:, j], start=True, stop=True).then_inc(kvT_done, 1)
                        pe.wait_ge(kv_copied, b)
                        for t in range(TB):
                            last = pe.matmul(kv_ps[:, t], ctxT[:, j, t * P:(t + 1) * P], wk[:], start=True, stop=True)
                        last.then_inc(kv_done, 1)
                        for t in range(TB):
                            pe.wait_ge(p_ready, b * TB + t + 1)
                            if t < 2:
                                pe.wait_ge(xnT_copied, b * TB)
                            else:
                                pe.wait_ge(pT_copied, b * TB + t - 1)
                            for k in range(KC):
                                last = pe.transpose(tr_ps[t % 2][:, k], p[:, t, k * P:(k + 1) * P], ident[:])
                            last.then_inc(pT_done, 1)
                        pe.wait_ge(kvT_copied, b + 1)
                        pe.wait_ge(kv_copied, b + 1)
                        pe.wait_ge(pT_copied, b * TB + TB)
                        for k in range(TB):
                            last = pe.matmul(kvT_ps[:], kv[:, k], pT[:, k], start=(k == 0), stop=(k == TB - 1))
                        last.then_inc(outT_done, 1)
                        pe.wait_ge(outT_copied, b + 1)
                        pe.wait_ge(logits_copied, b * TB)
                        for t in range(TB):
                            pe.matmul(sim_ps[t][:], outT[:, t * P:(t + 1) * P], kvT[:], start=True,
                                      stop=True).then_inc(sim_done, 1)
                        for t in range(TB):
                            pe.wait_ge(xn_done, b * TB + t + 1)
                            if t < 2:
                                pe.wait_ge(pT_copied, b * TB + TB)
                            else:
                                pe.wait_ge(xnT_copied, b * TB + t - 1)
                            for k in range(KC):
                                last = pe.transpose(tr_ps[t % 2][:, k], p[:, t, k * P:(k + 1) * P], ident[:])
                            last.then_inc(xnT_done, 1)
                            pe.wait_ge(xnT_copied, b * TB + t + 1)
                            pe.wait_ge(z_done, b * TB + TB)
                            for k in range(KC):
                                last = pe.matmul(sim_ps[t][:, 0:E], xnT[:, k * P:(k + 1) * P], wr[:, k],
                                                 start=(k == 0), stop=(k == KC - 1))
                            last.then_inc(logits_done, 1)

            @block.vector
            def _(dve):
                def settled():
                    dve.wait_ge(consts_in, 16 * NCONST)

                settled()
                with dve.Fori(0, B // 2) as bb:
                    for j in range(2):
                        b = bb * 2 + j

                        def split_lo(c):
                            e, (at, n, hi, lo), k = chunk_of(b, c)
                            dve.wait_ge(w_hi, b * PERB + c + 1)
                            rows = slice(64, P) if hi == lo else slice(0, P)
                            nc.vector.scalar_tensor_tensor(
                                W[rows, bass.ds(e, 1), lo:lo + n].rearrange("p a n -> p (a n)"), stage[rows, k, 0:n], WS,
                                W[rows, bass.ds(e, 1), hi:hi + n].rearrange("p a n -> p (a n)"), ALU.mult,
                                ALU.subtract).then_inc(w_lo, 1)

                        dve.wait_ge(x_in[j], bb * 16 + 16)
                        for t in range(TB):
                            nc.vector.bn_stats(st[:, t], xt[:, j, t]).then_inc(ln1_stat, 1)
                        for t in range(TB):
                            done = nc.snap(b * TB + t + 1)
                            settled()
                            dve.wait_ge(ln1_stat, done)
                            nc.vector.bn_aggr(mv[:, t], st[:, t]).then_inc(ln1_aggr, 1)
                        dve.wait_ge(ln1_aggr, b * TB + TB)
                        nc.vector.tensor_scalar_add(var[:], mv[:, :, 1], LN_EPS).then_inc(ln1_var, 1)
                        dve.wait_ge(outT_done, b)
                        dve.wait_ge(kv_done, b + 1)
                        nc.vector.tensor_tensor(kv[:], kv_ps[:], bk_row[:].unsqueeze(1).to_broadcast([P, TB, CD]),
                                                ALU.add).then_inc(kv_copied, 1)
                        dve.wait_ge(ln1_rstd, b + 1)
                        dve.wait_ge(xnT_done, b * TB)
                        for t in range(TB):
                            nc.vector.tensor_scalar(p[:, t], xt[:, j, t], mv[:, t, 0:1], rstd[:, t:t + 1],
                                                    ALU.subtract, ALU.mult).then_inc(p_ready, 1)
                        for c in range(0, 8):
                            split_lo(c)
                        for t in range(TB):
                            dve.wait_ge(sim_done, b * TB + t + 1)
                            nc.vector.bn_stats(st2[:, t], sim_ps[t][:]).then_inc(s_stat, 1)
                        for t in range(TB):
                            done = nc.snap(b * TB + t + 1)
                            settled()
                            dve.wait_ge(s_stat, done)
                            nc.vector.bn_aggr(mv2[:, t], st2[:, t]).then_inc(s_aggr, 1)
                        dve.wait_ge(s_aggr, b * TB + TB)
                        nc.vector.tensor_scalar(var2[:], mv2[:, :, 1], 1.0 / S, SIM_EPS, ALU.mult, ALU.add).then_inc(s_var, 1)
                        dve.wait_ge(s_rstd, b + 1)
                        nc.vector.tensor_scalar(coef[:], rstd2[:], float(S) ** -0.5, None, ALU.mult).then_inc(s_coef, 1)
                        dve.wait_ge(s_coef, b + 1)
                        nc.vector.scalar_tensor_tensor(nb[:], mv2[:, :, 0], -1.0, coef[:], ALU.mult, ALU.mult).then_inc(s_nb, 1)
                        for t in range(TB):
                            done = nc.snap(b * TB + t + 1)
                            settled()
                            dve.wait_ge(zg_done, done)
                            nc.vector.tensor_tensor_reduce(out=z[:, t], in0=z[:, t], in1=beta[:], scale=1.0, scalar=-BIG,
                                                           op0=ALU.add, op1=ALU.max, accum_out=mx[:, t:t + 1]).then_inc(zb_done, 1)
                            dve.wait_ge(zb_done, b * TB + t + 1)
                            nc.vector.tensor_scalar(nmx[:, t:t + 1], mx[:, t:t + 1], -1.0, None, ALU.mult).then_inc(nmx_done, 1)
                        for t in range(TB):
                            dve.wait_ge(exp_done, b * TB + t + 1)
                            nc.vector.reciprocal(rsum[:, t:t + 1], ssum[:, t:t + 1]).then_inc(rs_done, 1)
                            dve.wait_ge(rs_done, b * TB + t + 1)
                            nc.vector.scalar_tensor_tensor(xt[:, j, t], z[:, t], rsum[:, t:t + 1], xt[:, j, t],
                                                           ALU.mult, ALU.add).then_inc(x1_done, 1)
                            dve.wait_ge(x1_done, b * TB + t + 1)
                            nc.vector.bn_stats(st3[:, t], xt[:, j, t]).then_inc(ln2_stat, 1)
                        for t in range(TB):
                            done = nc.snap(b * TB + t + 1)
                            settled()
                            dve.wait_ge(ln2_stat, done)
                            nc.vector.bn_aggr(mv3[:, t], st3[:, t]).then_inc(ln2_aggr, 1)
                        dve.wait_ge(ln2_aggr, b * TB + TB)
                        nc.vector.tensor_scalar_add(var3[:], mv3[:, :, 1], LN_EPS).then_inc(ln2_var, 1)
                        for c in range(8, PERB):
                            split_lo(c)
                        dve.wait_ge(ln2_rstd, b + 1)
                        for t in range(TB):
                            nc.vector.tensor_scalar(p[:, t], xt[:, j, t], mv3[:, t, 0:1], rstd3[:, t:t + 1],
                                                    ALU.subtract, ALU.mult).then_inc(xn_done, 1)
                        for t in range(TB):
                            dve.wait_ge(hi_done, b * TB + t + 1)
                            nc.vector.scalar_tensor_tensor(pair[:, t % 2, H:2 * H], p[:, t], XS, pair[:, t % 2, 0:H],
                                                           ALU.mult, ALU.subtract).then_inc(lo_done, 1)
                            dve.wait_ge(logits_done, b * TB + t + 1)
                            nc.vector.tensor_copy(logits[:, bass.ds(b * TB + t, 1), :].rearrange("p a e -> p (a e)"),
                                                  sim_ps[t][:, 0:E]).then_inc(logits_copied, 1)


def routing(nc, d, W, logits, route):
    slots, weights, tokens, experts = route
    NQ = NT + QT
    with Scope(nc, "rt") as s:
        bias = s.sb("bias", [P, E])
        ex = s.sb("ex", [P, NT, E])
        sc = s.sb("sc", [P, NT, E])
        sb_ = s.sb("biased", [P, NT, E])
        top = s.sb("top", [P, NT, 8])
        topi = s.sb("topi", [P, NT, 8], U32)
        topf = s.sb("topf", [P, NT, 8])
        iota = s.sb("iota", [P, P])
        tokid = s.sb("tokid", [P, NT])
        before = s.sb("before", [P, P])
        ones = s.sb("ones", [P, P])
        mask = s.sb("mask", [P, NT, TOPK, E])
        tmp = s.sb("tmp", [P, NT, TOPK, E])
        M = s.sb("M", [P, NT, E])
        w4 = s.sb("w4", [P, NT, TOPK])
        wsum = s.sb("wsum", [P, NT])
        carry = s.sb("carry", [P, NT + 1, E])
        tiles_i = s.sb("tiles_i", [P, E], I32)
        tiles_s = s.sb("tiles_s", [P, E], I32)
        scan = s.sb("scan", [P, 2, E + E])
        pos = s.sb("pos", [P, NT, E])
        pos4 = s.sb("pos4", [P, NT, TOPK])
        pos4i = s.sb("pos4i", [P, NT, TOPK], I32)
        q4i = s.sb("q4i", [P, NT, TOPK], I32)
        r4i = s.sb("r4i", [P, NT, TOPK], I32)
        q4 = s.sb("q4", [P, NT, TOPK])
        r4 = s.sb("r4", [P, NT, TOPK])
        oneR = s.sb("oneR", [P, 2, TOPK, P], F16)
        oneQ = s.sb("oneQ", [P, 2, TOPK, NQ], F16)
        ge = s.sb("ge", [P, QT, E])
        ef = s.sb("ef", [P, NQ])
        CH = 2 * GU
        stage = s.sb("stage", [P, 2, CH])
        rank_ps = s.ps("rank_ps", [P, NT, E])
        count_ps = s.ps("count_ps", [P, NT, E])
        table_ps = s.ps("table_ps", [P, NQ])
        (bias_in, made, setup, ex_done, step, m_done, rank_done, count_done, w_hi, w_lo) = s.sems(
            "bias_in made setup ex_done step m_done rank_done count_done w_hi w_lo")
        w_in = s.sems("w_in0 w_in1")
        hot_done = s.sems("hot_done0 hot_done1")
        hot_used = s.sems("hot_used0 hot_used1")
        CHUNKS = [(0, CH, W_GU_HI, W_GU_LO), (CH, CH, W_GU_HI + CH, W_GU_LO + CH), (2 * CH, H, W_D0_HI, W_D0_LO),
                  (2 * CH + H, H, W_D1, W_D1)]
        with s.block() as block:
            @block.sync
            def _(sp):
                sp.dma_start(bias[:], d["ebias"].partition_broadcast(P)).then_inc(bias_in, 16)
                for c, (at, n, hi, lo) in enumerate(CHUNKS):
                    if c >= 2:
                        sp.wait_ge(w_lo, c - 1)
                    sp.dma_start(stage[:, c % 2, 0:n], d["wexp"][E, :, at:at + n]).then_inc(w_in[c % 2], 16)

            @block.gpsimd
            def _(pool):
                pool.iota(iota[:], pattern=[[1, P]], base=0, channel_multiplier=0, allow_small_or_imprecise_dtypes=True).then_inc(setup, 1)
                pool.iota(tokid[:], pattern=[[P, NT]], base=0, channel_multiplier=1, allow_small_or_imprecise_dtypes=True).then_inc(setup, 1)
                pool.memset(ones[:], 1.0).then_inc(made, 1)
                pool.wait_ge(made, 1)
                pool.affine_select(out=before[:], in_=ones[:], compare_op=ALU.is_gt, fill=0.0, base=0,
                                   pattern=[[1, P]], channel_multiplier=-1).then_inc(setup, 1)
                pool.memset(carry[:, 0], 0.0).then_inc(setup, 1)
                pool.memset(scan[:], 0.0).then_inc(setup, 1)

            @block.scalar
            def _(act):
                act.activation(ex[:], logits[:], ACT.Exp, scale=-1.0).then_inc(ex_done, 1)
                for c, (at, n, hi, lo) in enumerate(CHUNKS):
                    act.wait_ge(w_in[c % 2], 16 * (c // 2) + 16)
                    act.activation(W[:, E, hi:hi + n], stage[:, c % 2, 0:n], ACT.Copy, scale=WS).then_inc(w_hi, 1)

            @block.tensor
            def _(pe):
                pe.wait_ge(setup, 5)
                pe.wait_ge(m_done, 1)
                Mf, f = M[:].rearrange("p t e -> p (t e)"), "p t e -> p (t e)"
                pe.matmul(rank_ps[:].rearrange(f), before[:], Mf, start=True, stop=True).then_inc(rank_done, 1)
                pe.matmul(count_ps[:].rearrange(f), ones[:], Mf, start=True, stop=True).then_inc(count_done, 1)

                def place(i, j, first=False):
                    pe.wait_ge(hot_done[j], i + 1)
                    for k in range(TOPK):
                        last = pe.matmul(table_ps[:], oneR[:, j, k], oneQ[:, j, k], start=first and k == 0,
                                         stop=k == TOPK - 1, skip_group_check=True)
                    last.then_inc(hot_used[j], 1)

                place(0, 0, first=True)
                place(0, 1)
                with pe.Fori(1, NT // 2) as i:
                    for j in range(2):
                        place(i, j)

            @block.vector
            def _(dve):
                links = [0]

                def link(ins):
                    links[0] += 1
                    ins.then_inc(step, 1)
                    dve.wait_ge(step, links[0])

                def grid(a):
                    return a.unsqueeze(2).to_broadcast([P, NT, TOPK, E])

                v = nc.vector
                dve.wait_ge(bias_in, 16)
                dve.wait_ge(ex_done, 1)
                link(v.tensor_scalar_add(ex[:], ex[:], 1.0))
                link(v.reciprocal(sc[:], ex[:]))
                link(v.tensor_tensor(sb_[:], sc[:], bias[:].unsqueeze(1).to_broadcast([P, NT, E]), ALU.add))
                for t in range(NT):
                    last = v.max(top[:, t], sb_[:, t])
                link(last)
                for t in range(NT):
                    last = v.max_index(topi[:, t], top[:, t], sb_[:, t])
                link(last)
                link(v.tensor_copy(topf[:], topi[:]))
                dve.wait_ge(setup, 5)
                link(v.tensor_tensor(mask[:], topf[:, :, 0:TOPK].unsqueeze(3).to_broadcast([P, NT, TOPK, E]),
                                     iota[:, 0:E].unsqueeze(1).unsqueeze(1).to_broadcast([P, NT, TOPK, E]), ALU.is_equal))
                v.tensor_reduce(M[:], mask[:].rearrange("p t k e -> p t e k"), axis=AX.X, op=ALU.add).then_inc(m_done, 1)
                link(v.tensor_tensor(tmp[:], mask[:], grid(sc[:]), ALU.mult))
                link(v.tensor_reduce(w4[:], tmp[:], axis=AX.X, op=ALU.add))
                link(v.tensor_reduce(wsum[:], w4[:], axis=AX.X, op=ALU.add))
                link(v.tensor_scalar_add(wsum[:], wsum[:], 1e-20))
                link(v.reciprocal(wsum[:], wsum[:]))
                v.tensor_tensor(weights[:], w4[:], wsum[:].unsqueeze(2).to_broadcast([P, NT, TOPK]), ALU.mult)
                dve.wait_ge(count_done, 1)
                for t in range(NT):
                    link(v.tensor_tensor(carry[:, t + 1], carry[:, t], count_ps[:, t], ALU.add))
                link(v.tensor_scalar(tiles_i[:], carry[:, NT], float(P - 1), None, ALU.add))
                link(v.tensor_scalar(tiles_s[:], tiles_i[:], 7, None, ALU.logical_shift_right))
                link(v.tensor_scalar(scan[:, 0, E:E + 1], carry[:, 0, 0:1], float(NT), None, ALU.add))
                link(v.tensor_copy(scan[:, 0, E + 1:2 * E], tiles_s[:, 0:E - 1]))
                for n, k in enumerate((1, 2, 4, 8)):
                    a, b = scan[:, n % 2], scan[:, (n + 1) % 2]
                    link(v.tensor_tensor(b[:, E:2 * E], a[:, E:2 * E], a[:, E - k:2 * E - k], ALU.add))
                first = scan[:, 0, E:2 * E]
                dve.wait_ge(rank_done, 1)
                link(v.tensor_tensor(pos[:], rank_ps[:], carry[:, 0:NT], ALU.add))
                link(v.scalar_tensor_tensor(pos[:], first.unsqueeze(1).to_broadcast([P, NT, E]), float(P), pos[:],
                                            ALU.mult, ALU.add))
                link(v.tensor_tensor(tmp[:], mask[:], grid(pos[:]), ALU.mult))
                link(v.tensor_reduce(pos4[:], tmp[:], axis=AX.X, op=ALU.add))
                v.tensor_copy(slots[:], pos4[:])
                link(v.tensor_copy(pos4i[:], pos4[:]))
                v.tensor_scalar(q4i[:], pos4i[:], 7, None, ALU.logical_shift_right)
                link(v.tensor_scalar(r4i[:], pos4i[:], P - 1, None, ALU.bitwise_and))
                v.tensor_copy(q4[:], q4i[:])
                link(v.tensor_copy(r4[:], r4i[:]))
                with dve.Fori(0, NT // 2) as i:
                    for j in range(2):
                        t = i * 2 + j
                        dve.wait_ge(hot_used[j], i)
                        for k in range(TOPK):
                            v.tensor_scalar(oneR[:, j, k], iota[:], r4[:, bass.ds(t, 1), k], None, ALU.is_equal)
                            last = v.tensor_scalar(oneQ[:, j, k], iota[:, 0:NQ], q4[:, bass.ds(t, 1), k],
                                                   tokid[:, bass.ds(t, 1)], ALU.is_equal, ALU.mult)
                        last.then_inc(hot_done[j], 1)
                link(v.tensor_tensor(ge[:], iota[:, NT:NQ].unsqueeze(2).to_broadcast([P, QT, E]),
                                     first.unsqueeze(1).to_broadcast([P, QT, E]), ALU.is_ge))
                link(v.tensor_reduce(ef[:, NT:NQ], ge[:], axis=AX.X, op=ALU.add))
                link(v.memset(ef[:, 0:NT], float(E + 1)))
                link(v.tensor_scalar(ef[:], ef[:], -1.0, None, ALU.add))
                v.tensor_copy(experts[:], ef[:])
                for c, (at, n, hi, lo) in enumerate(CHUNKS):
                    dve.wait_ge(w_hi, c + 1)
                    rows = slice(64, P) if hi == lo else slice(0, P)
                    v.scalar_tensor_tensor(W[rows, E, lo:lo + n], stage[rows, c % 2, 0:n], WS, W[rows, E, hi:hi + n],
                                           ALU.mult, ALU.subtract).then_inc(w_lo, 1)
                for q in hot_used:
                    dve.wait_ge(q, NT // 2)
                v.tensor_copy(tokens[:, 0:NT], tokid[:])
                v.tensor_copy(tokens[:, NT:NQ], table_ps[:, NT:NQ])


def experts_ffn(nc, d, W, route, ident16):
    slots, weights, tokens, experts = route
    NQ = NT + QT
    with Scope(nc, "ex") as s:
        idx = s.sb("idx", [P, 2, 1], U32)
        xg = s.sb("xg", [P, 2, 2 * H], F16)
        xT = s.sb("xT", [P, 2, 2 * KC, P], F16)
        silu = s.sb("silu", [P, 2, EI])
        h = s.sb("h", [P, 2, EI])
        h16 = s.sb("h16", [P, 2, 4 * P], F16)
        hT = s.sb("hT", [P, 2, 4, P], F16)
        y = s.sb("y", [P, 2, H])
        xT_ps = [s.ps(f"xT_ps{j}", [P, 2 * KC, P], F16) for j in range(2)]
        gu_ps = [s.ps(f"gu_ps{j}", [P, GU]) for j in range(2)]
        hT_ps = [s.ps(f"hT_ps{j}", [P, 4, P], F16) for j in range(2)]
        y_ps = [s.ps(f"y_ps{j}", [P, H]) for j in range(2)]

        def pair(name):
            return s.sems(f"{name}0 {name}1")
        gathered = s.gpsimd_dma_sems("gathered0 gathered1")
        idx_set, xT_done, xT_copied, gu_done, silu_done, h_done, h16_done, hT_done, hT_copied, y_done, \
            y_copied, y_out = [pair(n) for n in "idx_set xT_done xT_copied gu_done silu_done h_done h16_done "
                               "hT_done hT_copied y_done y_copied y_out".split()]
        hi_done, started = s.sems("hi_done started")
        start = s.sb("start", [1, 1])

        def at(i, q):
            return i + q // 2, q % 2

        with s.block() as block:
            @block.gpsimd
            def _(pool):
                pool.memset(start[:], 0.0).then_inc(started, 1)
                with pool.Fori(0, NQ // 2) as i:
                    for j in range(2):
                        pool.wait_ge(xT_done[j], i)
                        nc.gpsimd.tensor_copy(idx[:, j], tokens[:, bass.ds(i * 2 + j, 1)]).then_inc(idx_set[j], 1)
                        done = nc.snap(i + 1)
                        pool.wait_ge(started, 1)
                        pool.wait_ge(idx_set[j], done)
                        pool.indirect_dma_start(xg[:, j], None, d["pairs"],
                                                bass.IndirectOffsetOnAxis(ap=idx[:, j], axis=0)).then_inc(gathered[j], 16)

            @block.tensor
            def _(pe):
                def load_x(i, j):
                    pe.wait_ge(gathered[j], i * 16 + 16)
                    pe.wait_ge(xT_copied[j], i)
                    for k in range(2 * KC):
                        last = pe.transpose(xT_ps[j][:, k], xg[:, j, k * P:(k + 1) * P], ident16[:])
                    last.then_inc(xT_done[j], 1)

                def expert_of(i, j):
                    return pe.value_load(experts[0:1, bass.ds(i * 2 + j, 1)], min_val=0, max_val=E)

                def cols(e, a, n):
                    return W[:, bass.ds(e, 1), a:a + n].rearrange("p a n -> p (a n)")

                def gate_up(i, j):
                    e = expert_of(i, j)
                    pe.wait_ge(xT_copied[j], i + 1)
                    pe.wait_ge(h_done[j], i)
                    n = 0
                    for k in range(KC):
                        for x, w in ((0, W_GU_HI), (0, W_GU_LO), (KC, W_GU_HI)):
                            last = pe.matmul(gu_ps[j][:], xT[:, j, x + k], cols(e, w + k * GU, GU),
                                             start=(n == 0), stop=(n == 3 * KC - 1))
                            n += 1
                    last.then_inc(gu_done[j], 1)

                def h_transposed(i, j):
                    pe.wait_ge(h16_done[j], i + 1)
                    pe.wait_ge(hT_copied[j], i)
                    for k in range(4):
                        last = pe.transpose(hT_ps[j][:, k], h16[:, j, k * P:(k + 1) * P], ident16[:])
                    last.then_inc(hT_done[j], 1)

                def down(i, j):
                    e = expert_of(i, j)
                    pe.wait_ge(hT_copied[j], i + 1)
                    pe.wait_ge(y_copied[j], i)
                    for n, (k, w) in enumerate(((0, W_D0_HI), (0, W_D0_LO), (1, W_D0_HI), (2, W_D1), (3, W_D1))):
                        last = pe.matmul(y_ps[j][:], hT[:, j, k], cols(e, w, H), start=(n == 0), stop=(n == 4))
                    last.then_inc(y_done[j], 1)

                load_x(*at(0, 0))
                gate_up(*at(0, 0))
                load_x(*at(0, 1))
                with pe.Fori(0, NQ // 2 - 1) as i:
                    for q in (1, 2):
                        gate_up(*at(i, q))
                        h_transposed(*at(i, q - 1))
                        load_x(*at(i, q + 1))
                        down(*at(i, q - 1))
                gate_up(*at(0, NQ - 1))
                for q in (NQ - 2, NQ - 1):
                    h_transposed(*at(0, q))
                    down(*at(0, q))

            @block.scalar
            def _(act):
                def copy_x(i, j):
                    act.wait_ge(xT_done[j], i + 1)
                    act.wait_ge(gu_done[j], i)
                    act.activation(xT[:, j], xT_ps[j][:], ACT.Copy).then_inc(xT_copied[j], 1)

                def gate(i, j):
                    act.wait_ge(gu_done[j], i + 1)
                    act.wait_ge(h_done[j], i)
                    act.activation(silu[:, j], gu_ps[j][:, 0:EI], ACT.Silu, scale=1.0 / (XS * WS)).then_inc(silu_done[j], 1)

                def copy_y(i, j):
                    act.wait_ge(y_done[j], i + 1)
                    act.wait_ge(y_out[j], i * 16)
                    act.activation(y[:, j], y_ps[j][:], ACT.Copy, scale=1.0 / (HS * WS)).then_inc(y_copied[j], 1)

                copy_x(*at(0, 0))
                gate(*at(0, 0))
                copy_x(*at(0, 1))
                with act.Fori(0, NQ // 2 - 1) as i:
                    for q in (1, 2):
                        gate(*at(i, q))
                        copy_x(*at(i, q + 1))
                        copy_y(*at(i, q - 1))
                gate(*at(0, NQ - 1))
                copy_y(*at(0, NQ - 2))
                copy_y(*at(0, NQ - 1))

            @block.vector
            def _(dve):
                v = nc.vector

                def inner(i, j):
                    dve.wait_ge(silu_done[j], i + 1)
                    v.scalar_tensor_tensor(h[:, j], gu_ps[j][:, EI:2 * EI], HS / (XS * WS), silu[:, j],
                                           ALU.mult, ALU.mult).then_inc(h_done[j], 1)
                    dve.wait_ge(h_done[j], i + 1)
                    dve.wait_ge(hT_done[j], i)
                    v.tensor_copy(h16[:, j, 0:P], h[:, j, 0:P])
                    v.tensor_copy(h16[:, j, 2 * P:3 * P].rearrange("p (a n) -> p a n", a=2),
                                  h[:, j, P:EI].unsqueeze(1).to_broadcast([P, 2, EI - P])).then_inc(hi_done, 1)
                    dve.wait_ge(hi_done, i * 2 + j + 1)
                    v.tensor_tensor(h16[:, j, P:2 * P], h[:, j, 0:P], h16[:, j, 0:P], ALU.subtract)
                    v.tensor_tensor(h16[:, j, 3 * P:3 * P + EI - P], h[:, j, P:EI], h16[:, j, 2 * P:2 * P + EI - P],
                                    ALU.subtract).then_inc(h16_done[j], 1)

                def copy_h(i, j):
                    dve.wait_ge(hT_done[j], i + 1)
                    dve.wait_ge(y_done[j], i)
                    v.tensor_copy(hT[:, j], hT_ps[j][:]).then_inc(hT_copied[j], 1)

                v.memset(h16[:], 0.0)
                inner(*at(0, 0))
                with dve.Fori(0, NQ // 2 - 1) as i:
                    for q in (1, 2):
                        copy_h(*at(i, q - 1))
                        inner(*at(i, q))
                copy_h(*at(0, NQ - 2))
                inner(*at(0, NQ - 1))
                copy_h(*at(0, NQ - 1))

            @block.sync
            def _(sp):
                with sp.Fori(0, NQ // 2) as i:
                    for j in range(2):
                        sp.wait_ge(y_copied[j], i + 1)
                        sp.dma_start(d["ys"][bass.ds((i * 2 + j) * P, P), :], y[:, j]).then_inc(y_out[j], 16)
                for j in range(2):
                    sp.wait_ge(y_out[j], 16 * NQ // 2)


def at(i, q):
    return i + q // 2, q % 2


L_WQ, L_WKV, L_WO, L_CTX = 0, KC * H, KC * H + 2 * H, 2 * KC * H + 2 * H
L_N = L_CTX + T
W1_N, W2_N = KC * FF, FF // P * H


def normalise_tile(nc, dve, ready, value, x, j, i, c, sems, xn):
    stat, aggr, var_set, rstd_set, xn_set, mhalf_set = sems
    value, done = nc.snap(value), nc.snap(i + 1)
    dve.wait_ge(mhalf_set, 1)
    dve.wait_ge(ready, value)
    nc.vector.bn_stats(c["st"][:, j], x).then_inc(stat[j], 1)
    dve.wait_ge(mhalf_set, 1)
    dve.wait_ge(stat[j], done)
    nc.vector.bn_aggr(c["mv"][:, j], c["st"][:, j]).then_inc(aggr[j], 1)
    dve.wait_ge(aggr[j], i + 1)
    nc.vector.tensor_scalar_add(c["var"][:, j:j + 1], c["mv"][:, j, 1:2], LN_EPS).then_inc(var_set[j], 1)
    dve.wait_ge(rstd_set[j], i + 1)
    nc.vector.tensor_scalar(xn, x, c["mv"][:, j, 0:1], c["rstd"][:, j:j + 1], ALU.subtract, ALU.mult).then_inc(xn_set[j], 1)


def combine(nc, d, route, xnT, L, ident16):
    slots, weights, tokens, experts = route
    CH = L_N // (NT // 2)
    with Scope(nc, "co") as s:
        idx = s.sb("idx", [P, 2, TOPK], U32)
        yk = s.sb("yk", [P, 2, TOPK, H])
        xa = s.sb("xa", [P, 2, H])
        xb = s.sb("xb", [P, 2, H])
        xn = s.sb("xn", [P, 2, H])
        pair = s.sb("pair", [P, 2, 2 * H], F16)
        stage = s.sb("stage", [P, CH])
        mhalf = s.sb("mhalf", [P, 1])
        c = {"st": s.sb("st", [P, 2, 6]), "mv": s.sb("mv", [P, 2, 2]), "var": s.sb("var", [P, 2]), "rstd": s.sb("rstd", [P, 2])}
        tr_ps = [s.ps(f"tr_ps{j}", [P, 2 * KC, P], F16) for j in range(2)]

        def duo(name):
            return s.sems(f"{name}0 {name}1")
        gathered = s.gpsimd_dma_sems("gathered0 gathered1")
        idx_set, x_in, acc, stat, aggr, var_set, rstd_set, xn_set, hi_set, lo_set, tr_done, tr_copied, x_out = [
            duo(n) for n in "idx_set x_in acc stat aggr var_set rstd_set xn_set hi_set lo_set tr_done "
            "tr_copied x_out".split()]
        mhalf_set, w_in, w_hi, w_lo = s.sems("mhalf_set w_in w_hi w_lo")
        with s.block() as block:
            @block.sync
            def _(sp):
                def load(i, j):
                    sp.wait_ge(x_out[j], 16 * i)
                    sp.dma_start(xa[:, j:j + 1], d["x1"][:, bass.ds(i * 2 + j, 1), :]).then_inc(x_in[j], 16)
                    sp.dma_start(xb[:, j], d["ys"][bass.ds((i * 2 + j) * P, P), :]).then_inc(x_in[j], 16)

                def store(i, j):
                    sp.wait_ge(xn_set[j], i + 1)
                    sp.dma_start(d["x2"][:, bass.ds(i * 2 + j, 1), :], xa[:, j:j + 1]).then_inc(x_out[j], 16)

                def split(i):
                    sp.wait_ge(w_lo, i)
                    sp.dma_start(stage[:], d["l1"][:, bass.ds(i * CH, CH)]).then_inc(w_in, 16)

                load(*at(0, 0))
                load(*at(0, 1))
                with sp.Fori(0, NT // 2 - 1) as i:
                    split(i)
                    for j in range(2):
                        store(i, j)
                        load(i + 1, j)
                split(NT // 2 - 1)
                for j in range(2):
                    store(NT // 2 - 1, j)
                for j in range(2):
                    sp.wait_ge(x_out[j], 16 * (NT // 2))

            @block.gpsimd
            def _(pool):
                def gather(i, j):
                    pool.wait_ge(acc[j], i * (TOPK + 1))
                    nc.gpsimd.tensor_copy(idx[:, j], slots[:, bass.ds(i * 2 + j, 1), :].rearrange("p a k -> p (a k)"))\
                        .then_inc(idx_set[j], 1)
                    done = nc.snap(i + 1)
                    pool.wait_ge(mhalf_set, 1)
                    pool.wait_ge(idx_set[j], done)
                    for k in range(TOPK):
                        pool.indirect_dma_start(yk[:, j, k], None, d["ys"],
                                                bass.IndirectOffsetOnAxis(ap=idx[:, j, k:k + 1], axis=0)).then_inc(gathered[j], 16)

                def power(i, j):
                    pool.wait_ge(var_set[j], i + 1)
                    nc.gpsimd.tensor_tensor(c["rstd"][:, j:j + 1], c["var"][:, j:j + 1], mhalf[:], ALU.pow).then_inc(rstd_set[j], 1)

                pool.memset(mhalf[:], -0.5).then_inc(mhalf_set, 1)
                pool.wait_ge(mhalf_set, 1)
                gather(*at(0, 0))
                with pool.Fori(0, NT // 2 - 1) as i:
                    for q in (0, 1):
                        gather(*at(i, q + 1))
                        power(*at(i, q))
                gather(*at(0, NT - 1))
                power(*at(0, NT - 2))
                power(*at(0, NT - 1))

            @block.scalar
            def _(act):
                with act.Fori(0, NT // 2) as i:
                    act.wait_ge(w_in, 16 * i + 16)
                    act.activation(L[:, 0, bass.ds(i * CH, CH)], stage[:], ACT.Copy, scale=WS).then_inc(w_hi, 1)
                    for j in range(2):
                        act.wait_ge(xn_set[j], i + 1)
                        act.wait_ge(tr_done[j], i)
                        act.activation(pair[:, j, 0:H], xn[:, j], ACT.Copy, scale=XS).then_inc(hi_set[j], 1)
                        act.wait_ge(tr_done[j], i + 1)
                        act.activation(xnT[:, :, :, bass.ds((i * 2 + j) * P, P)].rearrange("p s k n -> p (s k) n"),
                                       tr_ps[j][:], ACT.Copy).then_inc(tr_copied[j], 1)

            @block.tensor
            def _(pe):
                with pe.Fori(0, NT // 2) as i:
                    for j in range(2):
                        pe.wait_ge(lo_set[j], i + 1)
                        pe.wait_ge(tr_copied[j], i)
                        for k in range(2 * KC):
                            last = pe.transpose(tr_ps[j][:, k], pair[:, j, k * P:(k + 1) * P], ident16[:])
                        last.then_inc(tr_done[j], 1)

            @block.vector
            def _(dve):
                v = nc.vector
                with dve.Fori(0, NT // 2) as i:
                    for j in range(2):
                        dve.wait_ge(x_in[j], 32 * i + 32)
                        n = TOPK + 1
                        v.tensor_tensor(xa[:, j], xa[:, j], xb[:, j], ALU.add).then_inc(acc[j], 1)
                        dve.wait_ge(gathered[j], 16 * TOPK * (i + 1))
                        for k in range(TOPK):
                            dve.wait_ge(acc[j], i * n + k + 1)
                            v.scalar_tensor_tensor(xa[:, j], yk[:, j, k], weights[:, bass.ds(i * 2 + j, 1), k], xa[:, j],
                                                   ALU.mult, ALU.add).then_inc(acc[j], 1)
                        normalise_tile(nc, dve, acc[j], i * n + n, xa[:, j], j, i, c, (stat, aggr, var_set, rstd_set, xn_set, mhalf_set), xn[:, j])
                        dve.wait_ge(hi_set[j], i + 1)
                        v.scalar_tensor_tensor(pair[:, j, H:2 * H], xn[:, j], XS, pair[:, j, 0:H], ALU.mult,
                                               ALU.subtract).then_inc(lo_set[j], 1)
                    dve.wait_ge(w_hi, i + 1)
                    v.scalar_tensor_tensor(L[:, 1, bass.ds(i * CH, CH)], stage[:], WS, L[:, 0, bass.ds(i * CH, CH)],
                                           ALU.mult, ALU.subtract).then_inc(w_lo, 1)


NEG = -60000.0
BIGI = 16384.0
AS = 64.0


def attention1(nc, d, xnT, L, W1, AT):
    U = B * NG
    CH = W1_N // (U // 2)
    SCALE = 1.0 / (QS * QS * float(np.sqrt(HD)))
    with Scope(nc, "a1") as s:
        qk = s.sb("qk", [P, 4, S], F16)
        stk = s.sb("stk", [3 * HD + 1, 2, 2, HG, S], F16)
        vv = s.sb("vv", [P, 2, TB, P])
        pT = s.sb("pT", [P, 2, HG, S])
        rec = s.sb("rec", [P, S])
        o = s.sb("o", [P, S])
        mx = s.sb("mx", [P, 2, HG * TB])
        m16 = s.sb("m16", [P, HG * TB], F16)
        mT = s.sb("mT", [HG * TB, P], F16)
        ones = s.sb("ones", [P, HD])
        zero = s.sb("zero", [P, P], F16)
        bigI = s.sb("bigI", [P, P], F16)
        ident = s.sb("ident", [P, P], F16)
        hide = s.sb("hide", [P, P], F16)
        hideT = s.sb("hideT", [P, P], F16)
        stage = s.sb("stage", [P, CH])
        a_ps = s.ps("a_ps", [P, S])
        k_ps = s.ps("k_ps", [P, S])
        s_ps = [s.ps(f"s_ps{r}", [P, S]) for r in range(2)]
        sT_ps = [s.ps(f"sT_ps{r}", [P, S]) for r in range(2)]
        o_ps = s.ps("o_ps", [P, S])
        sum_ps = s.ps("sum_ps", [P, S])
        mT_ps = k_ps[0:HG * TB, 0:P // 2].bitcast(F16)

        def duo(name):
            return s.sems(f"{name}0 {name}1")
        (made, setup, q_done, k_done, v_done, qh, ql, kh, kl, v_copied, stacked, mrow_in, m16_set, mT_done, mT_copied,
         rec_done, o_done, ah, al, w_in, w_hi, w_lo) = s.sems(
            "made setup q_done k_done v_done qh ql kh kl v_copied stacked mrow_in m16_set mT_done mT_copied "
            "rec_done o_done ah al w_in w_hi w_lo")
        s_done, s_used, sT_done, sT_used, av_done = [duo(n) for n in "s_done s_used sT_done sT_used av_done".split()]
        NST = 4 * HG

        with s.block() as block:
            @block.gpsimd
            def _(pool):
                pool.memset(ones[:], 1.0).then_inc(setup, 1)
                pool.memset(zero[:], 0.0).then_inc(made, 1)
                pool.wait_ge(made, 1)

                def select(out, op, fill, base=0, cm=1, step=-1):
                    pool.affine_select(out=out, in_=zero[:], compare_op=op, fill=fill, base=base, pattern=[[step, P]],
                                       channel_multiplier=cm).then_inc(setup, 1)
                select(bigI[:], ALU.not_equal, BIGI)
                select(ident[:], ALU.not_equal, 1.0)
                select(hide[:], ALU.is_ge, NEG)
                select(hideT[:], ALU.is_ge, NEG, cm=-1, step=1)

            @block.sync
            def _(sp):
                def stack(i, j):
                    made, used = nc.snap(i * 2 + j + 1), nc.snap(i * TB)
                    sp.wait_ge(ql, made)
                    sp.wait_ge(kl, made)
                    sp.wait_ge(av_done[j], used)
                    for h in range(HG):
                        r = slice(h * HD, (h + 1) * HD)
                        sp.dma_start(stk[0:HD, j, 0, h], qk[r, 2]).then_inc(stacked, 16)
                        sp.dma_start(stk[0:HD, j, 1, h], qk[r, 1]).then_inc(stacked, 16)
                        sp.dma_start(stk[HD:2 * HD, j, :, h], qk[r, 0:2]).then_inc(stacked, 16)
                        sp.dma_start(stk[2 * HD:3 * HD, j, :, h], qk[r, 2:4]).then_inc(stacked, 16)

                def max_row(i, j):
                    sp.wait_ge(mT_copied, i * 2 + j + 1)
                    sp.dma_start(stk[3 * HD:3 * HD + 1, j, 0].rearrange("p h (t n) -> p (h t) n", t=TB),
                                 mT[:]).then_inc(mrow_in, 16)

                stack(*at(0, 0))
                stack(*at(0, 1))
                max_row(*at(0, 0))
                with sp.Fori(0, U // 2 - 1) as i:
                    sp.wait_ge(w_lo, i)
                    sp.dma_start(stage[:], d["w1"][:, bass.ds(i * CH, CH)]).then_inc(w_in, 16)
                    for q in (0, 1):
                        max_row(*at(i, q + 1))
                        stack(*at(i, q + 2))
                sp.wait_ge(w_lo, U // 2 - 1)
                sp.dma_start(stage[:], d["w1"][:, W1_N - CH:W1_N]).then_inc(w_in, 16)
                max_row(*at(0, U - 1))
                sp.wait_ge(mrow_in, 16 * U)

            @block.tensor
            def _(pe):
                def project(i, j, m_of=None):
                    u = i * 2 + j
                    col, row = u % NG * P, u // NG * S
                    pe.wait_ge(v_copied, u)
                    n = 0
                    for k in range(KC):
                        for w, x in ((0, 0), (0, 1), (1, 0)):
                            if n == 6 and m_of is not None:
                                maxima(*m_of)
                            last = pe.matmul(a_ps[:], L[:, w, bass.ds(col + L_WQ + k * H, P)], xnT[:, x, k, bass.ds(row, S)],
                                             start=(n == 0), stop=(n == 3 * KC - 1))
                            n += 1
                    last.then_inc(q_done, 1)
                    pe.wait_ge(kl, u)
                    pe.wait_ge(kh, u)
                    if m_of is not None:
                        pe.wait_ge(mT_copied, m_of[0] * 2 + m_of[1] + 1)
                    for n, (w, x) in enumerate(((0, 0), (0, 1), (1, 0))):
                        last = pe.matmul(k_ps[:], L[:, w, bass.ds(col + L_WKV, P)], L[:, x, bass.ds(row + L_CTX, S)],
                                         start=(n == 0), stop=(n == 2))
                    last.then_inc(k_done, 1)
                    pe.wait_ge(ql, u + 1)
                    for t in range(TB):
                        for n, (x, w) in enumerate(((0, 0), (0, 1), (1, 0))):
                            last = pe.matmul(a_ps[:, t * P:(t + 1) * P], L[:, x, bass.ds(row + L_CTX + t * P, P)],
                                             L[:, w, bass.ds(col + L_WKV + H, P)], start=(n == 0), stop=(n == 2))
                    last.then_inc(v_done, 1)

                def maxima(i, j):
                    pe.wait_ge(m16_set, i * 2 + j + 1)
                    pe.wait_ge(kl, i * 2 + j + 1)
                    pe.transpose(mT_ps, m16[:], ident[:]).then_inc(mT_done, 1)

                def first_pass(i, j, h):
                    u = i * 2 + j
                    if h == 0:
                        pe.wait_ge(stacked, (u + 1) * 16 * NST)
                    for t in range(TB):
                        n = u * 2 * HG + h * 2 + t // 2
                        pe.wait_ge(s_used[t % 2], n)
                        out = s_ps[t % 2]
                        pe.matmul(out[:, 0:(t + 1) * P], stk[0:3 * HD, j, 0, h, t * P:(t + 1) * P],
                                  stk[0:3 * HD, j, 1, h, 0:(t + 1) * P], start=True, stop=True)
                        pe.matmul(out[:, t * P:(t + 1) * P], bigI[:], hide[:], start=False, stop=True,
                                  skip_group_check=True).then_inc(s_done[t % 2], 1)

                def second_pass(i, j, t):
                    u = i * 2 + j
                    if t == 0:
                        pe.wait_ge(mrow_in, (u + 1) * 16)
                    for h in range(HG):
                        pe.wait_ge(sT_used[h % 2], u * 2 * TB + t * 2 + h // 2)
                        out = sT_ps[h % 2]
                        pe.matmul(out[:, 0:S - t * P], stk[:, j, 1, h, t * P:(t + 1) * P], stk[:, j, 0, h, t * P:S],
                                  start=True, stop=True)
                        pe.matmul(out[:, 0:P], bigI[:], hideT[:], start=False, stop=True,
                                  skip_group_check=True).then_inc(sT_done[h % 2], 1)

                def values(i, j, t):
                    u = i * 2 + j
                    for r in range(2):
                        pe.wait_ge(sT_used[r], u * 2 * TB + (t + 1) * 2)
                    if t == 0:
                        pe.wait_ge(o_done, u)
                        pe.wait_ge(v_copied, u + 1)
                    for out, what in ((o_ps, vv), (sum_ps, None)):
                        for h in range(HG):
                            r = slice(h * HD, (h + 1) * HD)
                            lhs = ones[:] if what is None else vv[:, j, t, r]
                            last = pe.matmul(out[r, t * P:S], lhs, pT[:, t % 2, h, t * P:S], start=(t == 0),
                                             stop=(t == TB - 1), tile_position=(0, h * HD), skip_group_check=True)
                    last.then_inc(av_done[j], 1)

                def region(now, nxt=None):
                    second_pass(*now, 0)
                    if nxt:
                        first_pass(*nxt, 0)
                    for t in range(1, TB):
                        second_pass(*now, t)
                        values(*now, t - 1)
                        if nxt:
                            first_pass(*nxt, t)
                    values(*now, TB - 1)

                pe.wait_ge(setup, 6)
                project(*at(0, 0))
                project(*at(0, 1))
                for h in range(HG):
                    first_pass(*at(0, 0), h)
                maxima(*at(0, 0))
                with pe.Fori(0, U // 2 - 1) as i:
                    for q in (0, 1):
                        region(at(i, q), at(i, q + 1))
                        project(*at(i, q + 2), m_of=at(i, q + 1))
                region(at(0, U - 2), at(0, U - 1))
                maxima(*at(0, U - 1))
                region(at(0, U - 1))

            @block.scalar
            def _(act):
                def project(i, j):
                    u = i * 2 + j
                    act.wait_ge(q_done, u + 1)
                    act.wait_ge(stacked, u * 16 * NST)
                    act.activation(qk[:, 2], a_ps[:], ACT.Copy, scale=QS / (XS * WS)).then_inc(qh, 1)
                    act.wait_ge(k_done, u + 1)
                    act.activation(qk[:, 1], k_ps[:], ACT.Copy, scale=QS / (WS * WS)).then_inc(kh, 1)
                    act.wait_ge(v_done, u + 1)
                    act.wait_ge(av_done[j], i * TB)
                    act.activation(vv[:, j].rearrange("p t n -> p (t n)"), a_ps[:], ACT.Copy, scale=1.0 / (WS * WS)).then_inc(v_copied, 1)

                def copy_max(i, j):
                    act.wait_ge(mT_done, i * 2 + j + 1)
                    act.wait_ge(mrow_in, 16 * (i * 2 + j))
                    act.activation(mT[:], mT_ps, ACT.Copy).then_inc(mT_copied, 1)

                def exps(i, j):
                    u = i * 2 + j
                    for t in range(TB):
                        if t == 0:
                            act.wait_ge(av_done[1 - j], (i + j) * TB)
                        elif t >= 2:
                            act.wait_ge(av_done[j], i * TB + t - 1)
                        for h in range(HG):
                            act.wait_ge(sT_done[h % 2], u * 2 * TB + t * 2 + h // 2 + 1)
                            act.activation(pT[:, t % 2, h, t * P:S], sT_ps[h % 2][:, 0:S - t * P], ACT.Exp, scale=SCALE)\
                                .then_inc(sT_used[h % 2], 1)

                def output(i, j):
                    u = i * 2 + j
                    act.wait_ge(o_done, u + 1)
                    act.activation(AT[:, 0, bass.ds(u % NG, 1), bass.ds(u // NG * S, S)].rearrange("p a n -> p (a n)"),
                                   o[:], ACT.Copy, scale=AS).then_inc(ah, 1)

                project(*at(0, 0))
                project(*at(0, 1))
                copy_max(*at(0, 0))
                with act.Fori(0, U // 2 - 1) as i:
                    act.wait_ge(w_in, 16 * i + 16)
                    act.activation(W1[:, 0, bass.ds(i * CH, CH)], stage[:], ACT.Copy, scale=WS).then_inc(w_hi, 1)
                    for q in (0, 1):
                        exps(*at(i, q))
                        copy_max(*at(i, q + 1))
                        output(*at(i, q))
                        project(*at(i, q + 2))
                act.wait_ge(w_in, 16 * (U // 2))
                act.activation(W1[:, 0, W1_N - CH:W1_N], stage[:], ACT.Copy, scale=WS).then_inc(w_hi, 1)
                exps(*at(0, U - 2))
                copy_max(*at(0, U - 1))
                output(*at(0, U - 2))
                exps(*at(0, U - 1))
                output(*at(0, U - 1))

            @block.vector
            def _(dve):
                v = nc.vector

                def project(i, j):
                    u = i * 2 + j
                    dve.wait_ge(qh, u + 1)
                    v.scalar_tensor_tensor(qk[:, 0], a_ps[:], QS / (XS * WS), qk[:, 2], ALU.mult, ALU.subtract).then_inc(ql, 1)
                    dve.wait_ge(kh, u + 1)
                    v.scalar_tensor_tensor(qk[:, 3], k_ps[:], QS / (WS * WS), qk[:, 1], ALU.mult, ALU.subtract).then_inc(kl, 1)

                def maxima(i, j):
                    u = i * 2 + j
                    for h in range(HG):
                        for t in range(TB):
                            dve.wait_ge(s_done[t % 2], u * 2 * HG + h * 2 + t // 2 + 1)
                            v.reduce_max(mx[:, j, h * TB + t:h * TB + t + 1], s_ps[t % 2][:, 0:(t + 1) * P], AX.X)\
                                .then_inc(s_used[t % 2], 1)
                    dve.wait_ge(s_used[1], (u + 1) * 2 * HG)
                    dve.wait_ge(s_used[0], (u + 1) * 2 * HG)
                    dve.wait_ge(mT_done, u)
                    v.tensor_scalar(m16[:], mx[:, j], -1.0 / WS, None, ALU.mult).then_inc(m16_set, 1)

                def output(i, j):
                    u = i * 2 + j
                    dve.wait_ge(av_done[j], (i + 1) * TB)
                    v.reciprocal(rec[:], sum_ps[:]).then_inc(rec_done, 1)
                    dve.wait_ge(rec_done, u + 1)
                    dve.wait_ge(ah, u)
                    v.tensor_tensor(o[:], o_ps[:], rec[:], ALU.mult).then_inc(o_done, 1)
                    dve.wait_ge(ah, u + 1)
                    v.scalar_tensor_tensor(AT[:, 1, bass.ds(u % NG, 1), bass.ds(u // NG * S, S)].rearrange("p a n -> p (a n)"),
                                           o[:], AS, AT[:, 0, bass.ds(u % NG, 1), bass.ds(u // NG * S, S)].rearrange("p a n -> p (a n)"),
                                           ALU.mult, ALU.subtract).then_inc(al, 1)

                v.memset(stk[3 * HD:3 * HD + 1, :, 1], WS).then_inc(setup, 1)
                project(*at(0, 0))
                project(*at(0, 1))
                maxima(*at(0, 0))
                with dve.Fori(0, U // 2 - 1) as i:
                    for q in (0, 1):
                        maxima(*at(i, q + 1))
                        output(*at(i, q))
                        project(*at(i, q + 2))
                    dve.wait_ge(w_hi, i + 1)
                    v.scalar_tensor_tensor(W1[:, 1, bass.ds(i * CH, CH)], stage[:], WS, W1[:, 0, bass.ds(i * CH, CH)],
                                           ALU.mult, ALU.subtract).then_inc(w_lo, 1)
                maxima(*at(0, U - 1))
                output(*at(0, U - 2))
                dve.wait_ge(w_hi, U // 2)
                v.scalar_tensor_tensor(W1[:, 1, W1_N - CH:W1_N], stage[:], WS, W1[:, 0, W1_N - CH:W1_N],
                                       ALU.mult, ALU.subtract).then_inc(w_lo, 1)
                output(*at(0, U - 1))


def project_out(nc, d, xnT, L, W2, AT, x3, ident16):
    CH = W2_N // (NT // 2)
    with Scope(nc, "po") as s:
        xn = s.sb("xn", [P, 2, H])
        pair = s.sb("pair", [P, 2, 2 * H], F16)
        stage = s.sb("stage", [P, CH])
        mhalf = s.sb("mhalf", [P, 1])
        c = {"st": s.sb("st", [P, 2, 6]), "mv": s.sb("mv", [P, 2, 2]), "var": s.sb("var", [P, 2]), "rstd": s.sb("rstd", [P, 2])}
        o_ps = [s.ps(f"o_ps{j}", [P, H]) for j in range(2)]
        tr_ps = [s.ps(f"tr_ps{j}", [P, 2 * KC, P], F16) for j in range(2)]

        def duo(name):
            return s.sems(f"{name}0 {name}1")
        o_done, x3_done, stat, aggr, var_set, rstd_set, xn_set, hi_set, lo_set, tr_done, tr_copied = [
            duo(n) for n in "o_done x3_done stat aggr var_set rstd_set xn_set hi_set lo_set tr_done tr_copied".split()]
        x_in, mhalf_set, w_in, w_hi, w_lo = s.sems("x_in mhalf_set w_in w_hi w_lo")
        with s.block() as block:
            @block.sync
            def _(sp):
                sp.dma_start(x3[:], d["x2"]).then_inc(x_in, 16)
                with sp.Fori(0, NT // 2) as i:
                    sp.wait_ge(w_lo, i)
                    sp.dma_start(stage[:], d["w2"][:, bass.ds(i * CH, CH)]).then_inc(w_in, 16)

            @block.gpsimd
            def _(pool):
                pool.memset(mhalf[:], -0.5).then_inc(mhalf_set, 1)
                pool.wait_ge(mhalf_set, 1)
                with pool.Fori(0, NT // 2) as i:
                    for j in range(2):
                        pool.wait_ge(var_set[j], i + 1)
                        nc.gpsimd.tensor_tensor(c["rstd"][:, j:j + 1], c["var"][:, j:j + 1], mhalf[:], ALU.pow)\
                            .then_inc(rstd_set[j], 1)

            @block.tensor
            def _(pe):
                def out(i, j):
                    pe.wait_ge(x3_done[j], i)
                    n = 0
                    for g in range(NG):
                        for x, w in ((0, 0), (0, 1), (1, 0)):
                            last = pe.matmul(o_ps[j][:], AT[:, x, g, bass.ds((i * 2 + j) * P, P)],
                                             L[:, w, L_WO + g * H:L_WO + (g + 1) * H], start=(n == 0), stop=(n == 3 * NG - 1))
                            n += 1
                    last.then_inc(o_done[j], 1)

                def transposes(i, j):
                    pe.wait_ge(lo_set[j], i + 1)
                    pe.wait_ge(tr_copied[j], i)
                    for k in range(2 * KC):
                        last = pe.transpose(tr_ps[j][:, k], pair[:, j, k * P:(k + 1) * P], ident16[:])
                    last.then_inc(tr_done[j], 1)

                out(*at(0, 0))
                out(*at(0, 1))
                with pe.Fori(0, NT // 2 - 1) as i:
                    for q in (0, 1):
                        out(*at(i, q + 2))
                        transposes(*at(i, q))
                transposes(*at(0, NT - 2))
                transposes(*at(0, NT - 1))

            @block.scalar
            def _(act):
                with act.Fori(0, NT // 2) as i:
                    act.wait_ge(w_in, 16 * i + 16)
                    act.activation(W2[:, 0, bass.ds(i * CH, CH)], stage[:], ACT.Copy, scale=WS).then_inc(w_hi, 1)
                    for j in range(2):
                        act.wait_ge(xn_set[j], i + 1)
                        act.wait_ge(tr_done[j], i)
                        act.activation(pair[:, j, 0:H], xn[:, j], ACT.Copy, scale=XS).then_inc(hi_set[j], 1)
                        act.wait_ge(tr_done[j], i + 1)
                        act.activation(xnT[:, :, :, bass.ds((i * 2 + j) * P, P)].rearrange("p s k n -> p (s k) n"),
                                       tr_ps[j][:], ACT.Copy).then_inc(tr_copied[j], 1)

            @block.vector
            def _(dve):
                v = nc.vector
                dve.wait_ge(x_in, 16)
                with dve.Fori(0, NT // 2) as i:
                    for j in range(2):
                        x = x3[:, bass.ds(i * 2 + j, 1), :].rearrange("p a n -> p (a n)")
                        dve.wait_ge(o_done[j], i + 1)
                        v.scalar_tensor_tensor(x, o_ps[j][:], 1.0 / (AS * WS), x, ALU.mult, ALU.add).then_inc(x3_done[j], 1)
                        normalise_tile(nc, dve, x3_done[j], i + 1, x, j, i, c, (stat, aggr, var_set, rstd_set, xn_set, mhalf_set), xn[:, j])
                        dve.wait_ge(hi_set[j], i + 1)
                        v.scalar_tensor_tensor(pair[:, j, H:2 * H], xn[:, j], XS, pair[:, j, 0:H], ALU.mult,
                                               ALU.subtract).then_inc(lo_set[j], 1)
                    dve.wait_ge(w_hi, i + 1)
                    v.scalar_tensor_tensor(W2[:, 1, bass.ds(i * CH, CH)], stage[:], WS, W2[:, 0, bass.ds(i * CH, CH)],
                                           ALU.mult, ALU.subtract).then_inc(w_lo, 1)


GS = 16.0


def ffn1(nc, d, xnT, W1, W2, x3):
    NF = FF // P
    W1c = W1[:, :, :].rearrange("p s (k f) -> p s k f", k=KC)
    W2c = W2[:, :, :].rearrange("p s (f n) -> p s f n", f=NF)
    with Scope(nc, "ff") as s:
        hq = s.sb("hq", [P, 2, S])
        qi = s.sb("qi", [P, 2, S], I16)
        a = s.sb("a", [P, 2, S])
        aT = s.sb("aT", [P, 2, 2, S], F16)
        h_ps = [s.ps(f"h_ps{j}", [P, S]) for j in range(2)]
        y_ps = [s.ps(f"y_ps{t}", [P, H]) for t in range(TB)]

        def duo(name):
            return s.sems(f"{name}0 {name}1")
        h_done, hq_done, qi_done, a_done, hi_done, lo_done, y_used = [
            duo(n) for n in "h_done hq_done qi_done a_done hi_done lo_done y_used".split()]
        out_added, stored = s.sems("out_added stored")
        with s.block() as block:
            @block.tensor
            def _(pe):
                with pe.Fori(0, B) as b:
                    def inner(i, j):
                        pe.wait_ge(hq_done[j], b * (NF // 2) + i)
                        n = 0
                        for k in range(KC):
                            for w, x in ((0, 0), (0, 1), (1, 0)):
                                last = pe.matmul(h_ps[j][:], W1c[:, w, k, bass.ds((i * 2 + j) * P, P)],
                                                 xnT[:, x, k, bass.ds(b * S, S)], start=(n == 0), stop=(n == 3 * KC - 1))
                                n += 1
                        last.then_inc(h_done[j], 1)

                    def outer(i, j, first=False, end=False):
                        pe.wait_ge(lo_done[j], b * (NF // 2) + i + 1)
                        if first:
                            pe.wait_ge(out_added, b * TB)
                        for t in range(TB):
                            for n, (x, w) in enumerate(((0, 0), (0, 1), (1, 0))):
                                last = pe.matmul(y_ps[t][:], aT[:, j, x, t * P:(t + 1) * P],
                                                 W2c[:, w, bass.ds(i * 2 + j, 1), :].rearrange("p a n -> p (a n)"),
                                                 start=first and n == 0, stop=end and n == 2, skip_group_check=True)
                        last.then_inc(y_used[j], 1)

                    inner(*at(0, 0))
                    inner(*at(0, 1))
                    outer(*at(0, 0), first=True)
                    with pe.Fori(0, NF // 2 - 1) as i:
                        for q in (1, 2):
                            inner(*at(i, q + 1))
                            outer(*at(i, q))
                    outer(*at(0, NF - 1), end=True)

            @block.scalar
            def _(act):
                with act.Fori(0, B) as b:
                    def scaled(i, j):
                        n = b * (NF // 2) + i
                        act.wait_ge(h_done[j], n + 1)
                        act.wait_ge(qi_done[j], n)
                        act.activation(hq[:, j], h_ps[j][:], ACT.Copy, scale=10.0 / (XS * WS)).then_inc(hq_done[j], 1)

                    def gelu(i, j):
                        n = b * (NF // 2) + i
                        act.wait_ge(qi_done[j], n + 1)
                        act.wait_ge(lo_done[j], n)
                        act.activation(a[:, j], qi[:, j], ACT.Gelu_apprx_tanh, scale=0.1).then_inc(a_done[j], 1)

                    with act.Fori(0, NF // 2) as i:
                        for j in range(2):
                            scaled(i, j)
                            gelu(i, j)

            @block.vector
            def _(dve):
                v = nc.vector
                with dve.Fori(0, B) as b:
                    with dve.Fori(0, NF // 2) as i:
                        n = b * (NF // 2) + i
                        for j in range(2):
                            dve.wait_ge(hq_done[j], n + 1)
                            dve.wait_ge(a_done[j], n)
                            v.tensor_scalar(qi[:, j], hq[:, j], -32768.0, 32767.0, ALU.max, ALU.min).then_inc(qi_done[j], 1)
                            dve.wait_ge(a_done[j], n + 1)
                            dve.wait_ge(y_used[j], n)
                            v.tensor_scalar(aT[:, j, 0], a[:, j], GS, None, ALU.mult).then_inc(hi_done[j], 1)
                            dve.wait_ge(hi_done[j], n + 1)
                            v.scalar_tensor_tensor(aT[:, j, 1], a[:, j], GS, aT[:, j, 0], ALU.mult, ALU.subtract)\
                                .then_inc(lo_done[j], 1)
                    dve.wait_ge(y_used[1], (b + 1) * (NF // 2))
                    for t in range(TB):
                        x = x3[:, bass.ds(b * TB + t, 1), :].rearrange("p a n -> p (a n)")
                        v.scalar_tensor_tensor(x, y_ps[t][:], 1.0 / (GS * WS), x, ALU.mult, ALU.add).then_inc(out_added, 1)

            @block.sync
            def _(sp):
                with sp.Fori(0, B) as b:
                    sp.wait_ge(out_added, (b + 1) * TB)
                    sp.dma_start(d["out"][:, bass.ds(b * TB, TB), :], x3[:, bass.ds(b * TB, TB), :]).then_inc(stored, 16)
                sp.wait_ge(stored, 16 * B)


def build(nc, d):
    d["x1"] = nc.dram_tensor("x1_rows", [P, NT, H], F32, kind="Internal").ap()
    d["x2"] = nc.dram_tensor("x2_rows", [P, NT, H], F32, kind="Internal").ap()
    d["pairs"] = nc.dram_tensor("normalised_rows", [T, 2 * H], F16, kind="Internal").ap()
    d["ys"] = nc.dram_tensor("expert_rows", [(NT + QT) * P, H], F32, kind="Internal").ap()
    with Scope(nc, "k") as s:
        ident16 = s.sb("ident16", [P, P], F16)
        route = (s.sb("slots", [P, NT, TOPK], U32), s.sb("weights", [P, NT, TOPK]),
                 s.sb("tokens", [P, NT + QT], U32), s.sb("experts", [P, NT + QT], I32))
        (made,) = s.sems("made")
        with Scope(nc, "l0") as l0:
            W = l0.sb("W", [P, E + 1, EW], F16)
            logits = l0.sb("logits", [P, NT, E])
            ident = l0.sb("ident", [P, P])
            with s.block() as block:
                @block.gpsimd
                def _(pool):
                    pool.memset(ident[:], 0.0).then_inc(made, 1)
                    pool.wait_ge(made, 1)
                    pool.affine_select(out=ident[:], in_=ident[:], compare_op=ALU.not_equal, fill=1.0, base=0,
                                       pattern=[[-1, P]], channel_multiplier=1).then_inc(made, 1)
                    pool.wait_ge(made, 2)
                    nc.gpsimd.tensor_copy(ident16[:], ident[:]).then_inc(made, 1)
                    pool.wait_ge(made, 3)
            attention0(nc, d, W, logits, ident)
            routing(nc, d, W, logits, route)
            experts_ffn(nc, d, W, route, ident16)
        xnT = s.sb("xnT", [P, 2, KC, T], F16)
        W1 = s.sb("W1", [P, 2, W1_N], F16)
        with Scope(nc, "l1") as l1:
            L = l1.sb("L", [P, 2, L_N], F16)
            AT = l1.sb("AT", [P, 2, NG, T], F16)
            combine(nc, d, route, xnT, L, ident16)
            attention1(nc, d, xnT, L, W1, AT)
            with Scope(nc, "f1") as f1:
                x3 = f1.sb("x3", [P, NT, H])
                W2 = f1.sb("W2", [P, 2, W2_N], F16)
                project_out(nc, d, xnT, L, W2, AT, x3, ident16)
                ffn1(nc, d, xnT, W1, W2, x3)


def layouts(x, ctx_512, L0_xattn_W_k, L0_xattn_b_k, L0_xattn_ln_gamma, L0_xattn_ln_beta, L0_ffn_router_w,
            L0_ffn_e_bias, L0_ffn_gate_up_proj, L0_ffn_down_proj, L0_ffn_shared_gate_w, L0_ffn_shared_up_w,
            L0_ffn_shared_down_w, L1_xattn_Wq, L1_xattn_Wkv_expand, L1_xattn_Wout, L1_ffn_W1, L1_ffn_W2):
    a = np.ascontiguousarray

    def rows(w):
        return a(w.reshape(-1, P, w.shape[1]).transpose(1, 0, 2))

    def expert(gate_up, down):
        dT = down.T
        last = dT[P:EI]
        return np.concatenate([rows(gate_up.T).reshape(P, -1), dT[0:P], np.concatenate([last, last])], axis=1)

    shared_gu = np.concatenate([L0_ffn_shared_gate_w, L0_ffn_shared_up_w])
    experts = [expert(L0_ffn_gate_up_proj[e], L0_ffn_down_proj[e]) for e in range(E)]
    return {
        "x": rows(x.reshape(T, H)),
        "ctxT": a(ctx_512.reshape(T, CD).T),
        "wkT": a(L0_xattn_W_k.T), "bk": a(L0_xattn_b_k), "bk_col": a(L0_xattn_b_k.reshape(CD, 1)),
        "gamma": a(L0_xattn_ln_gamma), "beta": a(L0_xattn_ln_beta),
        "wr": rows(L0_ffn_router_w.T), "ebias": a(L0_ffn_e_bias),
        "wexp": np.stack(experts + [expert(shared_gu, L0_ffn_shared_down_w)]),
        "l1": np.concatenate([rows(L1_xattn_Wq.T).reshape(P, -1), L1_xattn_Wkv_expand.T,
                              rows(L1_xattn_Wout.T).reshape(P, -1), ctx_512.reshape(T, CD).T], axis=1),
        "w1": rows(L1_ffn_W1.T).reshape(P, -1), "w2": rows(L1_ffn_W2.T).reshape(P, -1),
    }


def kernel(**inputs):
    import concourse.bacc as bacc
    from concourse.bass_utils import run_bass_kernel_spmd

    nc = bacc.Bacc("TRN2", target_bir_lowering=False, num_devices=1)
    arrays = layouts(**{name: np.asarray(a) for name, a in inputs.items()})
    d = {name: nc.dram_tensor(f"in_{name}", a.shape, mybir.dt.from_np(a.dtype), kind="ExternalInput").ap()
         for name, a in arrays.items()}
    d["out"] = nc.dram_tensor("out_rows", (P, NT, H), F32, kind="ExternalOutput").ap()
    build(nc, d)
    got = run_bass_kernel_spmd(nc, [{f"in_{name}": a for name, a in arrays.items()}], core_ids=[0]).results[0]["out_rows"]
    return np.ascontiguousarray(got.transpose(1, 0, 2)).reshape(B, S, H)
```

```python
from contextlib import ExitStack

import numpy as np

import concourse.bass as bass
from concourse import mybir

ACT = mybir.ActivationFunctionType
ALU = mybir.AluOpType
F32 = mybir.dt.float32
F16 = mybir.dt.float16
I16 = mybir.dt.int16
I32 = mybir.dt.int32
U32 = mybir.dt.uint32
AX = mybir.AxisListType

P = 128
B, S, H = 4, 512, 512
T = B * S
NT = T // P
TB = S // P
KC = H // P
CD = 128
E, TOPK, EI = 16, 4, 192
FF = 2048
NH, HD = 16, 32
HG = P // HD
NG = NH // HG

QT = T * TOPK // P + E
XS, WS, HS, QS = 2048.0, 256.0, 16.0, 16.0
LN_EPS, SIM_EPS = 1e-5, 1e-6
BIG = 3.0e38

GU = 2 * EI
W_GU_HI, W_GU_LO = 0, KC * GU
W_D0_HI, W_D0_LO = 2 * KC * GU, 2 * KC * GU + H
W_D1 = W_D0_LO + H
EW = W_D1 + H
EWF = KC * GU + 2 * H
CHUNK = 2 * GU
CHUNKS = [(0, CHUNK, W_GU_HI, W_GU_LO), (CHUNK, CHUNK, W_GU_HI + CHUNK, W_GU_LO + CHUNK), (2 * CHUNK, H, W_D0_HI, W_D0_LO),
          (2 * CHUNK + H, H, W_D1, W_D1)]


class Scope:

    def __init__(self, nc, stage):
        self.nc, self.stage, self.stack, self.made = nc, stage, ExitStack(), []

    def __enter__(self):
        return self

    def __exit__(self, *e):
        if self.made and e[0] is None:
            with self.nc.Block() as block:
                @block.sync
                def _(sp):
                    for sem in self.made:
                        sp.sem_clear(sem)
        return self.stack.__exit__(*e)

    def sb(self, name, shape, dt=F32):
        return self.stack.enter_context(self.nc.sbuf_tensor(f"{self.stage}_{name}", shape, dt))

    def ps(self, name, shape, dt=F32):
        return self.stack.enter_context(self.nc.psum_tensor(f"{self.stage}_{name}", shape, dt))

    def sems(self, names):
        made = [self.stack.enter_context(self.nc.semaphore(f"{self.stage}_{n}")) for n in names.split()]
        self.made += made
        return made

    def gpsimd_dma_sems(self, names):
        return [self.nc.alloc_semaphore(f"{self.stage}_{n}") for n in names.split()]

    def block(self):
        return self.nc.Block()


def attention0(nc, d, logits, ident):
    with Scope(nc, "a0") as s:
        wk = s.sb("wk", [P, CD])
        bk_col = s.sb("bk_col", [P, 1])
        bk_row = s.sb("bk_row", [P, CD])
        gamma = s.sb("gamma", [P, S])
        beta = s.sb("beta", [P, S])
        wr = s.sb("wr", [P, KC, E])
        xt = s.sb("xt", [P, NT, H])
        ctxT = s.sb("ctxT", [P, S])
        kv = s.sb("kv", [P, TB, CD])
        kvT = s.sb("kvT", [P, S])
        p = s.sb("p", [P, TB, H])
        pT = s.sb("pT", [P, KC, S])
        outT = s.sb("outT", [P, S])
        z = s.sb("z", [P, TB, S])
        xn = s.sb("xn", [P, TB, H])
        xnT = s.sb("xnT", [P, TB, H])
        pair = s.sb("pair", [P, TB, 2 * H], F16)
        mhalf = s.sb("mhalf", [P, TB])
        small = {n: s.sb(n, [P, TB, 6]) for n in ("st1", "st2", "st3")}
        small |= {n: s.sb(n, [P, TB, 2]) for n in ("mv1", "mv2", "mv3")}
        small |= {n: s.sb(n, [P, TB]) for n in ("var1", "var2", "var3", "rstd1", "rstd2", "rstd3")}
        coef = s.sb("coef", [P, TB])
        nb = s.sb("nb", [P, TB])
        mx = s.sb("mx", [P, TB])
        nmx = s.sb("nmx", [P, TB])
        ssum = s.sb("ssum", [P, TB])
        rsum = s.sb("rsum", [P, TB])

        kv_ps = s.ps("kv_ps", [P, TB, CD])
        kvT_ps = s.ps("kvT_ps", [P, S])
        tr_ps = [s.ps(f"tr_ps{i}", [P, KC, P]) for i in range(2)]
        sim_ps = [s.ps(f"sim_ps{i}", [P, S]) for i in range(TB)]

        (consts_in, x_first, x_rest, ctx_in, mhalf_set, kv_done, kvT_done, kv_copied, kvT_copied, stat1, aggr1, var1_set,
         rstd1_set, p_ready, pT_done, pT_copied, outT_done, outT_copied, sim_done, stat2, aggr2, var2_set, rstd2_set,
         coef_set, nb_set, z_done, zg_done, zb_done, nmx_done, exp_done, rs_done, x1_done, stat3, aggr3, var3_set,
         rstd3_set, xs_set, xn_done, hi_done, lo_done, xnT_done, xnT_copied, logits_done, logits_copied, x1_out) = s.sems(
            "consts_in x_first x_rest ctx_in mhalf_set kv_done kvT_done kv_copied kvT_copied stat1 aggr1 var1_set "
            "rstd1_set p_ready pT_done pT_copied outT_done outT_copied sim_done stat2 aggr2 var2_set rstd2_set "
            "coef_set nb_set z_done zg_done zb_done nmx_done exp_done rs_done x1_done stat3 aggr3 var3_set "
            "rstd3_set xs_set xn_done hi_done lo_done xnT_done xnT_copied logits_done logits_copied x1_out")
        pair_out = s.sems("pair_out0 pair_out1 pair_out2 pair_out3")
        NCONST = 6

        with s.block() as block:
            @block.sync
            def _(sp):
                def context(b):
                    sp.dma_start(ctxT[:], d["ctxT"][:, bass.ds(b * S, S)]).then_inc(ctx_in, 16)

                def store(b):
                    sp.wait_ge(x1_done, (b + 1) * TB)
                    sp.dma_start(d["x1"][:, bass.ds(b * TB, TB), :], xt[:, bass.ds(b * TB, TB), :]).then_inc(x1_out, 16)
                    for t in range(TB):
                        sp.wait_ge(lo_done, b * TB + t + 1)
                        sp.dma_start(d["pairs"][bass.ds((b * TB + t) * P, P), :], pair[:, t]).then_inc(pair_out[t], 16)

                sp.dma_start(xt[:, 0:TB], d["x"][:, 0:TB, :]).then_inc(x_first, 16)
                context(0)
                for dst, src in ((wk, d["wkT"]), (bk_col, d["bk_col"]), (gamma, d["gamma"].partition_broadcast(P)),
                                 (beta, d["beta"].partition_broadcast(P)), (bk_row, d["bk"].partition_broadcast(P)),
                                 (wr, d["wr"])):
                    sp.dma_start(dst[:], src).then_inc(consts_in, 16)
                sp.dma_start(xt[:, TB:NT], d["x"][:, TB:NT, :]).then_inc(x_rest, 16)
                with sp.Fori(0, B - 1) as b:
                    sp.wait_ge(kvT_done, b + 1)
                    sp.wait_ge(kv_done, b + 1)
                    context(b + 1)
                    store(b)
                store(B - 1)
                sp.wait_ge(x1_out, 16 * B)
                for q in pair_out:
                    sp.wait_ge(q, 16 * B)

            @block.gpsimd
            def _(pool):
                g = nc.gpsimd

                def power(n, b, var_set, rstd_set):
                    pool.wait_ge(var_set, b + 1)
                    g.tensor_tensor(small["rstd" + n][:], small["var" + n][:], mhalf[:], ALU.pow).then_inc(rstd_set, 1)

                def entry(b, more):
                    power("2", b, var2_set, rstd2_set)
                    if more:
                        power("1", b + 1, var1_set, rstd1_set)
                    for t in range(TB):
                        pool.wait_ge(z_done, b * TB + t + 1)
                        g.tensor_tensor(z[:, t], z[:, t], gamma[:], ALU.mult).then_inc(zg_done, 1)
                    power("3", b, var3_set, rstd3_set)
                    for t in range(TB):
                        pool.wait_ge(hi_done, b * TB + t + 1)
                        g.tensor_tensor(pair[:, t, H:2 * H], xn[:, t], pair[:, t, 0:H], ALU.subtract).then_inc(lo_done, 1)

                pool.memset(mhalf[:], -0.5).then_inc(mhalf_set, 1)
                pool.wait_ge(mhalf_set, 1)
                pool.wait_ge(consts_in, 16 * NCONST)
                power("1", 0, var1_set, rstd1_set)
                with pool.Fori(0, B - 1) as b:
                    entry(b, True)
                entry(B - 1, False)

            @block.scalar
            def _(act):
                def kvT_out(b):
                    act.wait_ge(kvT_done, b + 1)
                    act.wait_ge(sim_done, b * TB)
                    act.activation(kvT[:], kvT_ps[:], ACT.Identity, bias=bk_col[:, 0:1]).then_inc(kvT_copied, 1)

                def pT_out(b):
                    for t in range(TB):
                        act.wait_ge(pT_done, b * TB + t + 1)
                        act.wait_ge(outT_done, b)
                        act.activation(pT[:, :, t * P:(t + 1) * P], tr_ps[t % 2][:], ACT.Copy).then_inc(pT_copied, 1)

                def outT_out(b):
                    act.wait_ge(outT_done, b + 1)
                    act.wait_ge(sim_done, b * TB)
                    act.activation(outT[:], kvT_ps[:], ACT.Copy).then_inc(outT_copied, 1)

                def entry(b, more):
                    if more:
                        kvT_out(b + 1)
                    act.wait_ge(nb_set, b + 1)
                    act.wait_ge(x1_done, b * TB)
                    for t in range(TB):
                        act.activation(z[:, t], sim_ps[t][:], ACT.Identity, bias=nb[:, t:t + 1],
                                       scale=coef[:, t:t + 1]).then_inc(z_done, 1)
                    if more:
                        pT_out(b + 1)
                    for t in range(TB):
                        act.wait_ge(nmx_done, b * TB + t + 1)
                        act.activation(z[:, t], z[:, t], ACT.Exp, bias=nmx[:, t:t + 1],
                                       accum_out=ssum[:, t:t + 1]).then_inc(exp_done, 1)
                    if more:
                        outT_out(b + 1)
                    for t in range(TB):
                        act.wait_ge(xn_done, b * TB + t + 1)
                        act.wait_ge(pair_out[t], b * 16)
                        act.activation(pair[:, t, 0:H], xn[:, t], ACT.Copy).then_inc(hi_done, 1)
                        act.wait_ge(xnT_done, b * TB + t + 1)
                        act.wait_ge(logits_done, b * TB)
                        act.activation(xnT[:, t], tr_ps[t % 2][:], ACT.Copy).then_inc(xnT_copied, 1)
                    act.wait_ge(logits_done, (b + 1) * TB)
                    act.activation(logits[:, bass.ds(b * TB, TB), :], kv_ps[:, :, 0:E], ACT.Copy,
                                   scale=1.0 / XS).then_inc(logits_copied, 1)

                act.wait_ge(consts_in, 16 * NCONST)
                kvT_out(0)
                pT_out(0)
                outT_out(0)
                with act.Fori(0, B - 1) as b:
                    entry(b, True)
                entry(B - 1, False)

            @block.tensor
            def _(pe):
                def first(b, before):
                    pe.wait_ge(ctx_in, b * 16 + 16)
                    pe.wait_ge(outT_copied, b)
                    pe.matmul(kvT_ps[:], wk[:], ctxT[:], start=True, stop=True).then_inc(kvT_done, 1)
                    pe.wait_ge(logits_copied, before)
                    for t in range(TB):
                        last = pe.matmul(kv_ps[:, t], ctxT[:, t * P:(t + 1) * P], wk[:], start=True, stop=True)
                    last.then_inc(kv_done, 1)
                    for t in range(TB):
                        pe.wait_ge(p_ready, b * TB + t + 1)
                        if t < 2:
                            pe.wait_ge(xnT_copied, before * TB)
                        else:
                            pe.wait_ge(pT_copied, b * TB + t - 1)
                        for k in range(KC):
                            last = pe.transpose(tr_ps[t % 2][:, k], p[:, t, k * P:(k + 1) * P], ident[:])
                        last.then_inc(pT_done, 1)
                    pe.wait_ge(kvT_copied, b + 1)
                    pe.wait_ge(kv_copied, b + 1)
                    pe.wait_ge(pT_copied, b * TB + TB)
                    for k in range(TB):
                        last = pe.matmul(kvT_ps[:], kv[:, k], pT[:, k], start=(k == 0), stop=(k == TB - 1))
                    last.then_inc(outT_done, 1)
                    pe.wait_ge(outT_copied, b + 1)
                    pe.wait_ge(z_done, b * TB)
                    for t in range(TB):
                        pe.matmul(sim_ps[t][:], outT[:, t * P:(t + 1) * P], kvT[:], start=True,
                                  stop=True).then_inc(sim_done, 1)

                def second(b, ahead):
                    def transposes(t):
                        pe.wait_ge(xn_done, b * TB + t + 1)
                        if t < 2:
                            pe.wait_ge(pT_copied, ahead * TB)
                        else:
                            pe.wait_ge(xnT_copied, b * TB + t - 1)
                        for k in range(KC):
                            last = pe.transpose(tr_ps[t % 2][:, k], xn[:, t, k * P:(k + 1) * P], ident[:])
                        last.then_inc(xnT_done, 1)

                    transposes(0)
                    transposes(1)
                    pe.wait_ge(kv_copied, ahead)
                    for t in range(TB):
                        pe.wait_ge(xnT_copied, b * TB + t + 1)
                        for k in range(KC):
                            last = pe.matmul(kv_ps[:, t, 0:E], xnT[:, t, k * P:(k + 1) * P], wr[:, k],
                                             start=(k == 0), stop=(k == KC - 1))
                        last.then_inc(logits_done, 1)
                        if t + 2 < TB:
                            transposes(t + 2)

                pe.wait_ge(consts_in, 16 * NCONST)
                first(0, 0)
                with pe.Fori(0, B - 1) as b:
                    first(b + 1, b)
                    second(b, b + 2)
                second(B - 1, B)

            @block.vector
            def _(dve):
                v = nc.vector

                def aggregate(n, b, stat, aggr):
                    done = nc.snap(b + 1)
                    dve.wait_ge(consts_in, 16 * NCONST)
                    dve.wait_ge(stat, done)
                    for t in range(TB):
                        last = v.bn_aggr(small["mv" + n][:, t], small["st" + n][:, t])
                    last.then_inc(aggr, 1)
                    dve.wait_ge(aggr, b + 1)

                def mean_and_variance(b):
                    for t in range(TB):
                        x = xt[:, bass.ds(b * TB + t, 1), :].rearrange("p a n -> p (a n)")
                        last = v.bn_stats(small["st1"][:, t], x)
                    last.then_inc(stat1, 1)
                    aggregate("1", b, stat1, aggr1)
                    v.tensor_scalar_add(small["var1"][:], small["mv1"][:, :, 1], LN_EPS).then_inc(var1_set, 1)

                def normalise(b):
                    dve.wait_ge(kv_done, b + 1)
                    dve.wait_ge(outT_done, b)
                    v.tensor_tensor(kv[:], kv_ps[:], bk_row[:].unsqueeze(1).to_broadcast([P, TB, CD]), ALU.add)\
                        .then_inc(kv_copied, 1)
                    dve.wait_ge(rstd1_set, b + 1)
                    dve.wait_ge(pT_done, b * TB)
                    for t in range(TB):
                        v.tensor_scalar(p[:, t], xt[:, bass.ds(b * TB + t, 1), :].rearrange("p a n -> p (a n)"),
                                        small["mv1"][:, t, 0:1], small["rstd1"][:, t:t + 1], ALU.subtract, ALU.mult)\
                            .then_inc(p_ready, 1)

                def entry(b, more):
                    for t in range(TB):
                        dve.wait_ge(sim_done, b * TB + t + 1)
                        last = v.bn_stats(small["st2"][:, t], sim_ps[t][:])
                    last.then_inc(stat2, 1)
                    aggregate("2", b, stat2, aggr2)
                    v.tensor_scalar(small["var2"][:], small["mv2"][:, :, 1], 1.0 / S, SIM_EPS, ALU.mult, ALU.add)\
                        .then_inc(var2_set, 1)
                    if more:
                        mean_and_variance(b + 1)
                    dve.wait_ge(rstd2_set, b + 1)
                    v.tensor_scalar(coef[:], small["rstd2"][:], float(S) ** -0.5, None, ALU.mult).then_inc(coef_set, 1)
                    dve.wait_ge(coef_set, b + 1)
                    v.scalar_tensor_tensor(nb[:], small["mv2"][:, :, 0], -1.0, coef[:], ALU.mult, ALU.mult).then_inc(nb_set, 1)
                    if more:
                        normalise(b + 1)
                    for t in range(TB):
                        done = nc.snap(b * TB + t + 1)
                        dve.wait_ge(consts_in, 16 * NCONST)
                        dve.wait_ge(zg_done, done)
                        v.tensor_tensor_reduce(out=z[:, t], in0=z[:, t], in1=beta[:], scale=1.0, scalar=-BIG,
                                               op0=ALU.add, op1=ALU.max, accum_out=mx[:, t:t + 1]).then_inc(zb_done, 1)
                        dve.wait_ge(zb_done, b * TB + t + 1)
                        v.tensor_scalar(nmx[:, t:t + 1], mx[:, t:t + 1], -1.0, None, ALU.mult).then_inc(nmx_done, 1)

                    def statistics(t):
                        done = nc.snap(b * TB + t + 1)
                        dve.wait_ge(consts_in, 16 * NCONST)
                        dve.wait_ge(x1_done, done)
                        return v.bn_stats(small["st3"][:, t], xt[:, bass.ds(b * TB + t, 1), :].rearrange("p a n -> p (a n)"))

                    for t in range(TB):
                        dve.wait_ge(exp_done, b * TB + t + 1)
                        v.reciprocal(rsum[:, t:t + 1], ssum[:, t:t + 1]).then_inc(rs_done, 1)
                        if t > 0:
                            statistics(t - 1)
                        dve.wait_ge(rs_done, b * TB + t + 1)
                        x = xt[:, bass.ds(b * TB + t, 1), :].rearrange("p a n -> p (a n)")
                        v.scalar_tensor_tensor(x, z[:, t], rsum[:, t:t + 1], x, ALU.mult, ALU.add).then_inc(x1_done, 1)
                    statistics(TB - 1).then_inc(stat3, 1)
                    aggregate("3", b, stat3, aggr3)
                    v.tensor_scalar_add(small["var3"][:], small["mv3"][:, :, 1], LN_EPS).then_inc(var3_set, 1)
                    dve.wait_ge(rstd3_set, b + 1)
                    v.tensor_scalar(small["rstd3"][:], small["rstd3"][:], XS, None, ALU.mult).then_inc(xs_set, 1)
                    dve.wait_ge(xs_set, b + 1)
                    dve.wait_ge(xnT_done, b * TB)
                    dve.wait_ge(lo_done, b * TB)
                    for t in range(TB):
                        v.tensor_scalar(xn[:, t], xt[:, bass.ds(b * TB + t, 1), :].rearrange("p a n -> p (a n)"),
                                        small["mv3"][:, t, 0:1], small["rstd3"][:, t:t + 1], ALU.subtract, ALU.mult)\
                            .then_inc(xn_done, 1)

                dve.wait_ge(consts_in, 16 * NCONST)
                dve.wait_ge(x_first, 16)
                mean_and_variance(0)
                normalise(0)
                dve.wait_ge(x_rest, 16)
                with dve.Fori(0, B - 1) as b:
                    entry(b, True)
                entry(B - 1, False)


def routing(nc, d, W, logits, route):
    slots, weights, tokens, experts = route
    NQ = NT + QT
    with Scope(nc, "rt") as s:
        bias = s.sb("bias", [P, E])
        ex = s.sb("ex", [P, NT, E])
        sc = s.sb("sc", [P, NT, E])
        sb_ = s.sb("biased", [P, NT, E])
        top = s.sb("top", [P, NT, 8])
        topi = s.sb("topi", [P, NT, 8], U32)
        topf = s.sb("topf", [P, NT, 8])
        iota = s.sb("iota", [P, P])
        tokid = s.sb("tokid", [P, NT])
        before = s.sb("before", [P, P])
        ones = s.sb("ones", [P, P])
        mask = s.sb("mask", [P, NT, TOPK, E])
        tmp = s.sb("tmp", [P, NT, TOPK, E])
        M = s.sb("M", [P, NT, E])
        w4 = s.sb("w4", [P, NT, TOPK])
        wsum = s.sb("wsum", [P, NT])
        carry = s.sb("carry", [P, NT + 1, E])
        tiles_i = s.sb("tiles_i", [P, E], I32)
        tiles_s = s.sb("tiles_s", [P, E], I32)
        scan = s.sb("scan", [P, 2, E + E])
        pos = s.sb("pos", [P, NT, E])
        pos4 = s.sb("pos4", [P, NT, TOPK])
        pos4i = s.sb("pos4i", [P, NT, TOPK], I32)
        q4i = s.sb("q4i", [P, NT, TOPK], I32)
        r4i = s.sb("r4i", [P, NT, TOPK], I32)
        q4 = s.sb("q4", [P, NT, TOPK])
        r4 = s.sb("r4", [P, NT, TOPK])
        oneR = s.sb("oneR", [P, 2, TOPK, P], F16)
        oneQ = s.sb("oneQ", [P, 2, TOPK, NQ], F16)
        ge = s.sb("ge", [P, QT, E])
        ef = s.sb("ef", [P, NQ])
        stage = s.sb("stage", [P, 2, CHUNK])
        rank_ps = s.ps("rank_ps", [P, NT, E])
        count_ps = s.ps("count_ps", [P, NT, E])
        table_ps = s.ps("table_ps", [P, NQ])
        (bias_in, made, setup, ex_done, step, m_done, rank_done, count_done, w_hi, w_lo) = s.sems(
            "bias_in made setup ex_done step m_done rank_done count_done w_hi w_lo")
        w_in = s.sems("w_in0 w_in1")
        hot_done = s.sems("hot_done0 hot_done1")
        hot_used = s.sems("hot_used0 hot_used1")
        with s.block() as block:
            @block.sync
            def _(sp):
                sp.dma_start(bias[:], d["ebias"].partition_broadcast(P)).then_inc(bias_in, 16)
                for c, (at, n, hi, lo) in enumerate(CHUNKS):
                    if c >= 2:
                        sp.wait_ge(w_lo, c - 1)
                    sp.dma_start(stage[:, c % 2, 0:n], d["wexp"][E, :, at:at + n]).then_inc(w_in[c % 2], 16)

            @block.gpsimd
            def _(pool):
                pool.iota(iota[:], pattern=[[1, P]], base=0, channel_multiplier=0, allow_small_or_imprecise_dtypes=True).then_inc(setup, 1)
                pool.iota(tokid[:], pattern=[[P, NT]], base=0, channel_multiplier=1, allow_small_or_imprecise_dtypes=True).then_inc(setup, 1)
                pool.memset(ones[:], 1.0).then_inc(made, 1)
                pool.wait_ge(made, 1)
                pool.affine_select(out=before[:], in_=ones[:], compare_op=ALU.is_gt, fill=0.0, base=0,
                                   pattern=[[1, P]], channel_multiplier=-1).then_inc(setup, 1)
                pool.memset(carry[:, 0], 0.0).then_inc(setup, 1)
                pool.memset(scan[:], 0.0).then_inc(setup, 1)

            @block.scalar
            def _(act):
                act.activation(ex[:], logits[:], ACT.Exp, scale=-1.0).then_inc(ex_done, 1)
                for c, (at, n, hi, lo) in enumerate(CHUNKS):
                    act.wait_ge(w_in[c % 2], 16 * (c // 2) + 16)
                    act.activation(W[:, E, hi:hi + n], stage[:, c % 2, 0:n], ACT.Copy, scale=WS).then_inc(w_hi, 1)

            @block.tensor
            def _(pe):
                pe.wait_ge(setup, 5)
                pe.wait_ge(m_done, 1)
                Mf, f = M[:].rearrange("p t e -> p (t e)"), "p t e -> p (t e)"
                pe.matmul(rank_ps[:].rearrange(f), before[:], Mf, start=True, stop=True).then_inc(rank_done, 1)
                pe.matmul(count_ps[:].rearrange(f), ones[:], Mf, start=True, stop=True).then_inc(count_done, 1)

                def place(i, j, first=False):
                    pe.wait_ge(hot_done[j], i + 1)
                    for k in range(TOPK):
                        last = pe.matmul(table_ps[:], oneR[:, j, k], oneQ[:, j, k], start=first and k == 0,
                                         stop=k == TOPK - 1, skip_group_check=True)
                    last.then_inc(hot_used[j], 1)

                place(0, 0, first=True)
                place(0, 1)
                with pe.Fori(1, NT // 2) as i:
                    for j in range(2):
                        place(i, j)

            @block.vector
            def _(dve):
                links = [0]

                def link(ins):
                    links[0] += 1
                    ins.then_inc(step, 1)
                    dve.wait_ge(step, links[0])

                def grid(a):
                    return a.unsqueeze(2).to_broadcast([P, NT, TOPK, E])

                v = nc.vector
                dve.wait_ge(bias_in, 16)
                dve.wait_ge(ex_done, 1)
                link(v.tensor_scalar_add(ex[:], ex[:], 1.0))
                link(v.reciprocal(sc[:], ex[:]))
                link(v.tensor_tensor(sb_[:], sc[:], bias[:].unsqueeze(1).to_broadcast([P, NT, E]), ALU.add))
                for t in range(NT):
                    last = v.max(top[:, t], sb_[:, t])
                link(last)
                for t in range(NT):
                    last = v.max_index(topi[:, t], top[:, t], sb_[:, t])
                link(last)
                link(v.tensor_copy(topf[:], topi[:]))
                dve.wait_ge(setup, 5)
                link(v.tensor_tensor(mask[:], topf[:, :, 0:TOPK].unsqueeze(3).to_broadcast([P, NT, TOPK, E]),
                                     iota[:, 0:E].unsqueeze(1).unsqueeze(1).to_broadcast([P, NT, TOPK, E]), ALU.is_equal))
                v.tensor_reduce(M[:], mask[:].rearrange("p t k e -> p t e k"), axis=AX.X, op=ALU.add).then_inc(m_done, 1)
                link(v.tensor_tensor(tmp[:], mask[:], grid(sc[:]), ALU.mult))
                link(v.tensor_reduce(w4[:], tmp[:], axis=AX.X, op=ALU.add))
                link(v.tensor_reduce(wsum[:], w4[:], axis=AX.X, op=ALU.add))
                link(v.tensor_scalar_add(wsum[:], wsum[:], 1e-20))
                link(v.reciprocal(wsum[:], wsum[:]))
                v.tensor_tensor(weights[:], w4[:], wsum[:].unsqueeze(2).to_broadcast([P, NT, TOPK]), ALU.mult)
                dve.wait_ge(count_done, 1)
                for t in range(NT):
                    link(v.tensor_tensor(carry[:, t + 1], carry[:, t], count_ps[:, t], ALU.add))
                link(v.tensor_scalar(tiles_i[:], carry[:, NT], float(P - 1), None, ALU.add))
                link(v.tensor_scalar(tiles_s[:], tiles_i[:], 7, None, ALU.logical_shift_right))
                link(v.tensor_scalar(scan[:, 0, E:E + 1], carry[:, 0, 0:1], float(NT), None, ALU.add))
                link(v.tensor_copy(scan[:, 0, E + 1:2 * E], tiles_s[:, 0:E - 1]))
                for n, k in enumerate((1, 2, 4, 8)):
                    a, b = scan[:, n % 2], scan[:, (n + 1) % 2]
                    link(v.tensor_tensor(b[:, E:2 * E], a[:, E:2 * E], a[:, E - k:2 * E - k], ALU.add))
                first = scan[:, 0, E:2 * E]
                dve.wait_ge(rank_done, 1)
                link(v.tensor_tensor(pos[:], rank_ps[:], carry[:, 0:NT], ALU.add))
                link(v.scalar_tensor_tensor(pos[:], first.unsqueeze(1).to_broadcast([P, NT, E]), float(P), pos[:],
                                            ALU.mult, ALU.add))
                link(v.tensor_tensor(tmp[:], mask[:], grid(pos[:]), ALU.mult))
                link(v.tensor_reduce(pos4[:], tmp[:], axis=AX.X, op=ALU.add))
                v.tensor_copy(slots[:], pos4[:])
                link(v.tensor_copy(pos4i[:], pos4[:]))
                v.tensor_scalar(q4i[:], pos4i[:], 7, None, ALU.logical_shift_right)
                link(v.tensor_scalar(r4i[:], pos4i[:], P - 1, None, ALU.bitwise_and))
                v.tensor_copy(q4[:], q4i[:])
                link(v.tensor_copy(r4[:], r4i[:]))
                with dve.Fori(0, NT // 2) as i:
                    for j in range(2):
                        t = i * 2 + j
                        dve.wait_ge(hot_used[j], i)
                        for k in range(TOPK):
                            v.tensor_scalar(oneR[:, j, k], iota[:], r4[:, bass.ds(t, 1), k], None, ALU.is_equal)
                            last = v.tensor_scalar(oneQ[:, j, k], iota[:, 0:NQ], q4[:, bass.ds(t, 1), k],
                                                   tokid[:, bass.ds(t, 1)], ALU.is_equal, ALU.mult)
                        last.then_inc(hot_done[j], 1)
                link(v.tensor_tensor(ge[:], iota[:, NT:NQ].unsqueeze(2).to_broadcast([P, QT, E]),
                                     first.unsqueeze(1).to_broadcast([P, QT, E]), ALU.is_ge))
                link(v.tensor_reduce(ef[:, NT:NQ], ge[:], axis=AX.X, op=ALU.add))
                link(v.memset(ef[:, 0:NT], float(E + 1)))
                link(v.tensor_scalar(ef[:], ef[:], -1.0, None, ALU.add))
                v.tensor_copy(experts[:], ef[:])
                for c, (at, n, hi, lo) in enumerate(CHUNKS):
                    dve.wait_ge(w_hi, c + 1)
                    rows = slice(64, P) if hi == lo else slice(0, P)
                    v.scalar_tensor_tensor(W[rows, E, lo:lo + n], stage[rows, c % 2, 0:n], WS, W[rows, E, hi:hi + n],
                                           ALU.mult, ALU.subtract).then_inc(w_lo, 1)
                for q in hot_used:
                    dve.wait_ge(q, NT // 2)
                v.tensor_copy(tokens[:, 0:NT], tokid[:])
                v.tensor_copy(tokens[:, NT:NQ], table_ps[:, NT:NQ])


def experts_ffn(nc, d, W, route, ident16):
    slots, weights, tokens, experts = route
    NQ = NT + QT
    with Scope(nc, "ex") as s:
        idx = s.sb("idx", [P, 2, 1], U32)
        xg = s.sb("xg", [P, 2, 2 * H], F16)
        xT = s.sb("xT", [P, 2, 2 * KC, P], F16)
        silu = s.sb("silu", [P, 2, EI])
        h = s.sb("h", [P, 2, EI])
        h16 = s.sb("h16", [P, 2, 4 * P], F16)
        hT = s.sb("hT", [P, 2, 4, P], F16)
        y = s.sb("y", [P, 2, H])
        stage = s.sb("stage", [P, len(CHUNKS), CHUNK])
        xT_ps = [s.ps(f"xT_ps{j}", [P, 2 * KC, P], F16) for j in range(2)]
        gu_ps = [s.ps(f"gu_ps{j}", [P, GU]) for j in range(2)]
        hT_ps = [s.ps(f"hT_ps{j}", [P, 4, P], F16) for j in range(2)]
        y_ps = [s.ps(f"y_ps{j}", [P, H]) for j in range(2)]

        def pair(name):
            return s.sems(f"{name}0 {name}1")
        gathered = s.gpsimd_dma_sems("gathered0 gathered1")
        idx_set, xT_done, xT_copied, gu_done, silu_done, h_done, h16_done, hT_done, hT_copied, y_done, \
            y_copied, y_out = [pair(n) for n in "idx_set xT_done xT_copied gu_done silu_done h_done h16_done "
                               "hT_done hT_copied y_done y_copied y_out".split()]
        hi_done, started, w_hi, w_lo = s.sems("hi_done started w_hi w_lo")
        w_in = s.sems("w_in0 w_in1 w_in2 w_in3")
        NC = len(CHUNKS)
        start = s.sb("start", [1, 1])

        def at(i, q):
            return i + q // 2, q % 2

        with s.block() as block:
            @block.gpsimd
            def _(pool):
                pool.memset(start[:], 0.0).then_inc(started, 1)
                with pool.Fori(0, NQ // 2) as i:
                    for j in range(2):
                        pool.wait_ge(xT_done[j], i)
                        nc.gpsimd.tensor_copy(idx[:, j], tokens[:, bass.ds(i * 2 + j, 1)]).then_inc(idx_set[j], 1)
                        done = nc.snap(i + 1)
                        pool.wait_ge(started, 1)
                        pool.wait_ge(idx_set[j], done)
                        pool.indirect_dma_start(xg[:, j], None, d["pairs"],
                                                bass.IndirectOffsetOnAxis(ap=idx[:, j], axis=0)).then_inc(gathered[j], 16)

            @block.tensor
            def _(pe):
                def load_x(i, j):
                    pe.wait_ge(gathered[j], i * 16 + 16)
                    pe.wait_ge(xT_copied[j], i)
                    for k in range(2 * KC):
                        last = pe.transpose(xT_ps[j][:, k], xg[:, j, k * P:(k + 1) * P], ident16[:])
                    last.then_inc(xT_done[j], 1)

                def expert_of(i, j):
                    return pe.value_load(experts[0:1, bass.ds(i * 2 + j, 1)], min_val=0, max_val=E)

                def split_of(e):
                    return (e + 1) % (E + 1) * NC + 1

                def cols(e, a, n):
                    return W[:, bass.ds(e, 1), a:a + n].rearrange("p a n -> p (a n)")

                def gate_up(i, j):
                    e = expert_of(i, j)
                    pe.wait_ge(w_lo, split_of(e))
                    pe.wait_ge(xT_copied[j], i + 1)
                    pe.wait_ge(h_done[j], i)
                    n = 0
                    for k in range(KC):
                        for x, w in ((0, W_GU_HI), (0, W_GU_LO), (KC, W_GU_HI)):
                            last = pe.matmul(gu_ps[j][:], xT[:, j, x + k], cols(e, w + k * GU, GU),
                                             start=(n == 0), stop=(n == 3 * KC - 1))
                            n += 1
                    last.then_inc(gu_done[j], 1)

                def h_transposed(i, j):
                    pe.wait_ge(h16_done[j], i + 1)
                    pe.wait_ge(hT_copied[j], i)
                    for k in range(4):
                        last = pe.transpose(hT_ps[j][:, k], h16[:, j, k * P:(k + 1) * P], ident16[:])
                    last.then_inc(hT_done[j], 1)

                def down(i, j):
                    e = expert_of(i, j)
                    pe.wait_ge(hT_copied[j], i + 1)
                    pe.wait_ge(y_copied[j], i)
                    for n, (k, w) in enumerate(((0, W_D0_HI), (0, W_D0_LO), (1, W_D0_HI), (2, W_D1), (3, W_D1))):
                        last = pe.matmul(y_ps[j][:], hT[:, j, k], cols(e, w, H), start=(n == 0), stop=(n == 4))
                    last.then_inc(y_done[j], 1)

                load_x(*at(0, 0))
                gate_up(*at(0, 0))
                load_x(*at(0, 1))
                with pe.Fori(0, NQ // 2 - 1) as i:
                    for q in (1, 2):
                        gate_up(*at(i, q))
                        h_transposed(*at(i, q - 1))
                        load_x(*at(i, q + 1))
                        down(*at(i, q - 1))
                gate_up(*at(0, NQ - 1))
                for q in (NQ - 2, NQ - 1):
                    h_transposed(*at(0, q))
                    down(*at(0, q))

            @block.scalar
            def _(act):
                def copy_x(i, j):
                    act.wait_ge(xT_done[j], i + 1)
                    act.wait_ge(gu_done[j], i)
                    act.activation(xT[:, j], xT_ps[j][:], ACT.Copy).then_inc(xT_copied[j], 1)

                def gate(i, j):
                    act.wait_ge(gu_done[j], i + 1)
                    act.wait_ge(h_done[j], i)
                    act.activation(silu[:, j], gu_ps[j][:, 0:EI], ACT.Silu, scale=1.0 / (XS * WS)).then_inc(silu_done[j], 1)

                def copy_y(i, j):
                    act.wait_ge(y_done[j], i + 1)
                    act.wait_ge(y_out[j], i * 16)
                    act.activation(y[:, j], y_ps[j][:], ACT.Copy, scale=1.0 / (HS * WS)).then_inc(y_copied[j], 1)

                def split(e, c):
                    at, n, hi, lo = CHUNKS[c]
                    act.wait_ge(w_in[c], 16 * e + 16)
                    act.activation(W[:, bass.ds(e, 1), hi:hi + n].rearrange("p a n -> p (a n)"), stage[:, c, 0:n],
                                   ACT.Copy, scale=WS).then_inc(w_hi, 1)

                def step(i, q, splits=False):
                    gate(*at(i, q))
                    copy_x(*at(i, q + 1))
                    if splits:
                        split(i, 2 * q - 2)
                        split(i, 2 * q - 1)
                    copy_y(*at(i, q - 1))

                copy_x(*at(0, 0))
                gate(*at(0, 0))
                copy_x(*at(0, 1))
                with act.Fori(0, E) as i:
                    for q in (1, 2):
                        step(i, q, splits=True)
                with act.Fori(E, NQ // 2 - 1) as i:
                    for q in (1, 2):
                        step(i, q)
                gate(*at(0, NQ - 1))
                copy_y(*at(0, NQ - 2))
                copy_y(*at(0, NQ - 1))

            @block.vector
            def _(dve):
                v = nc.vector

                def inner(i, j):
                    dve.wait_ge(silu_done[j], i + 1)
                    v.scalar_tensor_tensor(h[:, j], gu_ps[j][:, EI:2 * EI], HS / (XS * WS), silu[:, j],
                                           ALU.mult, ALU.mult).then_inc(h_done[j], 1)
                    dve.wait_ge(h_done[j], i + 1)
                    dve.wait_ge(hT_done[j], i)
                    v.tensor_copy(h16[:, j, 0:P], h[:, j, 0:P])
                    v.tensor_copy(h16[:, j, 2 * P:3 * P].rearrange("p (a n) -> p a n", a=2),
                                  h[:, j, P:EI].unsqueeze(1).to_broadcast([P, 2, EI - P])).then_inc(hi_done, 1)
                    dve.wait_ge(hi_done, i * 2 + j + 1)
                    v.tensor_tensor(h16[:, j, P:2 * P], h[:, j, 0:P], h16[:, j, 0:P], ALU.subtract)
                    v.tensor_tensor(h16[:, j, 3 * P:3 * P + EI - P], h[:, j, P:EI], h16[:, j, 2 * P:2 * P + EI - P],
                                    ALU.subtract).then_inc(h16_done[j], 1)

                def copy_h(i, j):
                    dve.wait_ge(hT_done[j], i + 1)
                    dve.wait_ge(y_done[j], i)
                    v.tensor_copy(hT[:, j], hT_ps[j][:]).then_inc(hT_copied[j], 1)

                def split(e, c):
                    at, n, hi, lo = CHUNKS[c]
                    dve.wait_ge(w_hi, e * NC + c + 1)
                    rows = slice(64, P) if hi == lo else slice(0, P)
                    v.scalar_tensor_tensor(W[rows, bass.ds(e, 1), lo:lo + n].rearrange("p a n -> p (a n)"),
                                           stage[rows, c, 0:n], WS, W[rows, bass.ds(e, 1), hi:hi + n]
                                           .rearrange("p a n -> p (a n)"), ALU.mult, ALU.subtract).then_inc(w_lo, 1)

                def step(i, q, splits=False):
                    copy_h(*at(i, q - 1))
                    inner(*at(i, q))
                    if splits:
                        split(i, 2 * q - 2)
                        split(i, 2 * q - 1)

                v.memset(h16[:], 0.0).then_inc(w_lo, 1)
                inner(*at(0, 0))
                with dve.Fori(0, E) as i:
                    for q in (1, 2):
                        step(i, q, splits=True)
                with dve.Fori(E, NQ // 2 - 1) as i:
                    for q in (1, 2):
                        step(i, q)
                copy_h(*at(0, NQ - 2))
                inner(*at(0, NQ - 1))
                copy_h(*at(0, NQ - 1))

            @block.sync
            def _(sp):
                def load(e, c):
                    at, n, hi, lo = CHUNKS[c]
                    sp.dma_start(stage[:, c, 0:n], d["wexp"][bass.ds(e, 1), :, at:at + n].rearrange("a p n -> p (a n)"))\
                        .then_inc(w_in[c], 16)

                def store(i, j):
                    sp.wait_ge(y_copied[j], i + 1)
                    sp.dma_start(d["ys"][bass.ds((i * 2 + j) * P, P), :], y[:, j]).then_inc(y_out[j], 16)

                for c in range(NC):
                    load(0, c)
                with sp.Fori(0, E - 1) as i:
                    for j in range(2):
                        for c in (2 * j, 2 * j + 1):
                            sp.wait_ge(w_lo, i * NC + c + 2)
                            load(i + 1, c)
                        store(i, j)
                with sp.Fori(E - 1, NQ // 2) as i:
                    for j in range(2):
                        store(i, j)
                for j in range(2):
                    sp.wait_ge(y_out[j], 16 * NQ // 2)


def at(i, q):
    return i + q // 2, q % 2


L_WQ, L_WKV, L_WO, L_CTX = 0, KC * H, KC * H + 2 * H, 2 * KC * H + 2 * H
L_N = L_CTX + T
W1_N, W2_N = KC * FF, FF // P * H


def normalise_tile(nc, dve, ready, value, x, j, i, c, sems, xn):
    stat, aggr, var_set, rstd_set, xn_set, mhalf_set = sems
    value, done = nc.snap(value), nc.snap(i + 1)
    dve.wait_ge(mhalf_set, 1)
    dve.wait_ge(ready, value)
    nc.vector.bn_stats(c["st"][:, j], x).then_inc(stat[j], 1)
    dve.wait_ge(mhalf_set, 1)
    dve.wait_ge(stat[j], done)
    nc.vector.bn_aggr(c["mv"][:, j], c["st"][:, j]).then_inc(aggr[j], 1)
    dve.wait_ge(aggr[j], i + 1)
    nc.vector.tensor_scalar_add(c["var"][:, j:j + 1], c["mv"][:, j, 1:2], LN_EPS).then_inc(var_set[j], 1)
    dve.wait_ge(rstd_set[j], i + 1)
    nc.vector.tensor_scalar(xn, x, c["mv"][:, j, 0:1], c["rstd"][:, j:j + 1], ALU.subtract, ALU.mult).then_inc(xn_set[j], 1)


def combine(nc, d, route, xnT, L, ident16):
    slots, weights, tokens, experts = route
    CH = L_N // (NT // 2)
    with Scope(nc, "co") as s:
        idx = s.sb("idx", [P, 2, TOPK], U32)
        yk = s.sb("yk", [P, 2, TOPK, H])
        xa = s.sb("xa", [P, 2, H])
        xb = s.sb("xb", [P, 2, H])
        xn = s.sb("xn", [P, 2, H])
        pair = s.sb("pair", [P, 2, 2 * H], F16)
        stage = s.sb("stage", [P, CH])
        mhalf = s.sb("mhalf", [P, 1])
        c = {"st": s.sb("st", [P, 2, 6]), "mv": s.sb("mv", [P, 2, 2]), "var": s.sb("var", [P, 2]), "rstd": s.sb("rstd", [P, 2])}
        tr_ps = [s.ps(f"tr_ps{j}", [P, 2 * KC, P], F16) for j in range(2)]

        def duo(name):
            return s.sems(f"{name}0 {name}1")
        gathered = s.gpsimd_dma_sems("gathered0 gathered1")
        idx_set, x_in, acc, stat, aggr, var_set, rstd_set, xn_set, hi_set, lo_set, tr_done, tr_copied, x_out = [
            duo(n) for n in "idx_set x_in acc stat aggr var_set rstd_set xn_set hi_set lo_set tr_done "
            "tr_copied x_out".split()]
        mhalf_set, w_in, w_hi, w_lo = s.sems("mhalf_set w_in w_hi w_lo")
        with s.block() as block:
            @block.sync
            def _(sp):
                def load(i, j):
                    sp.wait_ge(x_out[j], 16 * i)
                    sp.dma_start(xa[:, j:j + 1], d["x1"][:, bass.ds(i * 2 + j, 1), :]).then_inc(x_in[j], 16)
                    sp.dma_start(xb[:, j], d["ys"][bass.ds((i * 2 + j) * P, P), :]).then_inc(x_in[j], 16)

                def store(i, j):
                    sp.wait_ge(xn_set[j], i + 1)
                    sp.dma_start(d["x2"][:, bass.ds(i * 2 + j, 1), :], xa[:, j:j + 1]).then_inc(x_out[j], 16)

                def split(i):
                    sp.wait_ge(w_lo, i)
                    sp.dma_start(stage[:], d["l1"][:, bass.ds(i * CH, CH)]).then_inc(w_in, 16)

                load(*at(0, 0))
                load(*at(0, 1))
                with sp.Fori(0, NT // 2 - 1) as i:
                    split(i)
                    for j in range(2):
                        store(i, j)
                        load(i + 1, j)
                split(NT // 2 - 1)
                for j in range(2):
                    store(NT // 2 - 1, j)
                for j in range(2):
                    sp.wait_ge(x_out[j], 16 * (NT // 2))

            @block.gpsimd
            def _(pool):
                def gather(i, j):
                    pool.wait_ge(acc[j], i * (TOPK + 1))
                    nc.gpsimd.tensor_copy(idx[:, j], slots[:, bass.ds(i * 2 + j, 1), :].rearrange("p a k -> p (a k)"))\
                        .then_inc(idx_set[j], 1)
                    done = nc.snap(i + 1)
                    pool.wait_ge(mhalf_set, 1)
                    pool.wait_ge(idx_set[j], done)
                    for k in range(TOPK):
                        pool.indirect_dma_start(yk[:, j, k], None, d["ys"],
                                                bass.IndirectOffsetOnAxis(ap=idx[:, j, k:k + 1], axis=0)).then_inc(gathered[j], 16)

                def power(i, j):
                    pool.wait_ge(var_set[j], i + 1)
                    nc.gpsimd.tensor_tensor(c["rstd"][:, j:j + 1], c["var"][:, j:j + 1], mhalf[:], ALU.pow).then_inc(rstd_set[j], 1)

                pool.memset(mhalf[:], -0.5).then_inc(mhalf_set, 1)
                pool.wait_ge(mhalf_set, 1)
                gather(*at(0, 0))
                with pool.Fori(0, NT // 2 - 1) as i:
                    for q in (0, 1):
                        gather(*at(i, q + 1))
                        power(*at(i, q))
                gather(*at(0, NT - 1))
                power(*at(0, NT - 2))
                power(*at(0, NT - 1))

            @block.scalar
            def _(act):
                with act.Fori(0, NT // 2) as i:
                    act.wait_ge(w_in, 16 * i + 16)
                    act.activation(L[:, 0, bass.ds(i * CH, CH)], stage[:], ACT.Copy, scale=WS).then_inc(w_hi, 1)
                    for j in range(2):
                        act.wait_ge(xn_set[j], i + 1)
                        act.wait_ge(tr_done[j], i)
                        act.activation(pair[:, j, 0:H], xn[:, j], ACT.Copy, scale=XS).then_inc(hi_set[j], 1)
                        act.wait_ge(tr_done[j], i + 1)
                        act.activation(xnT[:, :, :, bass.ds((i * 2 + j) * P, P)].rearrange("p s k n -> p (s k) n"),
                                       tr_ps[j][:], ACT.Copy).then_inc(tr_copied[j], 1)

            @block.tensor
            def _(pe):
                with pe.Fori(0, NT // 2) as i:
                    for j in range(2):
                        pe.wait_ge(lo_set[j], i + 1)
                        pe.wait_ge(tr_copied[j], i)
                        for k in range(2 * KC):
                            last = pe.transpose(tr_ps[j][:, k], pair[:, j, k * P:(k + 1) * P], ident16[:])
                        last.then_inc(tr_done[j], 1)

            @block.vector
            def _(dve):
                v = nc.vector
                with dve.Fori(0, NT // 2) as i:
                    for j in range(2):
                        dve.wait_ge(x_in[j], 32 * i + 32)
                        n = TOPK + 1
                        v.tensor_tensor(xa[:, j], xa[:, j], xb[:, j], ALU.add).then_inc(acc[j], 1)
                        dve.wait_ge(gathered[j], 16 * TOPK * (i + 1))
                        for k in range(TOPK):
                            dve.wait_ge(acc[j], i * n + k + 1)
                            v.scalar_tensor_tensor(xa[:, j], yk[:, j, k], weights[:, bass.ds(i * 2 + j, 1), k], xa[:, j],
                                                   ALU.mult, ALU.add).then_inc(acc[j], 1)
                        normalise_tile(nc, dve, acc[j], i * n + n, xa[:, j], j, i, c, (stat, aggr, var_set, rstd_set, xn_set, mhalf_set), xn[:, j])
                        dve.wait_ge(hi_set[j], i + 1)
                        v.scalar_tensor_tensor(pair[:, j, H:2 * H], xn[:, j], XS, pair[:, j, 0:H], ALU.mult,
                                               ALU.subtract).then_inc(lo_set[j], 1)
                    dve.wait_ge(w_hi, i + 1)
                    v.scalar_tensor_tensor(L[:, 1, bass.ds(i * CH, CH)], stage[:], WS, L[:, 0, bass.ds(i * CH, CH)],
                                           ALU.mult, ALU.subtract).then_inc(w_lo, 1)


NEG = -60000.0
BIGI = 16384.0
AS = 64.0


def attention1(nc, d, xnT, L, W1, AT):
    U = B * NG
    CH = W1_N // U
    SCALE = 1.0 / (QS * QS * float(np.sqrt(HD)))
    with Scope(nc, "a1") as s:
        qk = s.sb("qk", [P, 2, 4, S], F16)
        NS = 4
        stk = s.sb("stk", [3 * HD + 1, NS, 2, HG, S], F16)
        vv = s.sb("vv", [P, 2, TB, P])
        pT = s.sb("pT", [P, 2, HG, S])
        rec = s.sb("rec", [P, S])
        o = s.sb("o", [P, S])
        mx = s.sb("mx", [P, 2, HG * TB])
        m16 = s.sb("m16", [P, HG * TB], F16)
        mT = s.sb("mT", [HG * TB, P], F16)
        ones = s.sb("ones", [P, HD])
        zero = s.sb("zero", [P, P], F16)
        bigI = s.sb("bigI", [P, P], F16)
        ident = s.sb("ident", [P, P], F16)
        hide = s.sb("hide", [P, P], F16)
        hideT = s.sb("hideT", [P, P], F16)
        stage = s.sb("stage", [P, CH])
        a_ps = s.ps("a_ps", [P, S])
        k_ps = s.ps("k_ps", [P, S])
        s_ps = [s.ps(f"s_ps{r}", [P, S]) for r in range(2)]
        sT_ps = [s.ps(f"sT_ps{r}", [P, S]) for r in range(2)]
        o_ps = s.ps("o_ps", [P, S])
        sum_ps = s.ps("sum_ps", [P, S])
        mT_ps = k_ps[0:HG * TB, 0:P // 2].bitcast(F16)

        def duo(name):
            return s.sems(f"{name}0 {name}1")
        (made, setup, row_set, q_done, k_done, v_done, qh, ql, kh, kl, v_copied, mrow_in, m16_set, mT_done, mT_copied,
         rec_done, o_done, ah, al, w_in, w_hi, w_lo) = s.sems(
            "made setup row_set q_done k_done v_done qh ql kh kl v_copied mrow_in m16_set mT_done mT_copied "
            "rec_done o_done ah al w_in w_hi w_lo")
        s_done, s_used, sT_done, sT_used, av_done, stacked = [
            duo(n) for n in "s_done s_used sT_done sT_used av_done stacked".split()]
        NST = 3 * HG

        def slot(i, j):
            return (i % (NS // 2)) * 2 + j

        with s.block() as block:
            @block.gpsimd
            def _(pool):
                pool.memset(ones[:], 1.0).then_inc(setup, 1)
                pool.memset(zero[:], 0.0).then_inc(made, 1)
                pool.wait_ge(made, 1)

                def select(out, op, fill, base=0, cm=1, step=-1):
                    pool.affine_select(out=out, in_=zero[:], compare_op=op, fill=fill, base=base, pattern=[[step, P]],
                                       channel_multiplier=cm).then_inc(setup, 1)
                select(bigI[:], ALU.not_equal, BIGI)
                select(ident[:], ALU.not_equal, 1.0)
                select(hide[:], ALU.is_ge, NEG)
                select(hideT[:], ALU.is_ge, NEG, cm=-1, step=1)
                pool.wait_ge(setup, 5)
                pool.memset(stk[3 * HD:3 * HD + 1, :, 1], WS).then_inc(row_set, 1)

            @block.sync
            def _(sp):
                def stack(i, j):
                    made = nc.snap(i * 2 + j + 1)
                    sp.wait_ge(ql, made)
                    sp.wait_ge(kl, made)
                    for h in range(HG):
                        r = slice(h * HD, (h + 1) * HD)
                        for part, which in enumerate((slice(0, 3, 2), slice(1, 3), slice(0, 4, 3))):
                            sp.dma_start(stk[part * HD:(part + 1) * HD, bass.ds(slot(i, j), 1), :, h]
                                         .rearrange("p a w n -> p (a w) n"), qk[r, j, which]).then_inc(stacked[j], 16)

                def max_row(i, j):
                    sp.wait_ge(mT_copied, i * 2 + j + 1)
                    sp.dma_start(stk[3 * HD:3 * HD + 1, bass.ds(slot(i, j), 1), 0].rearrange("p a h (t n) -> p (a h t) n", t=TB),
                                 mT[:]).then_inc(mrow_in, 16)

                def load(u):
                    sp.wait_ge(w_lo, u)
                    sp.dma_start(stage[:], d["w1"][:, bass.ds(u * CH, CH)]).then_inc(w_in, 16)

                def step(i, q, last=False):
                    load(i * 2 + q)
                    max_row(*at(i, q + 1))
                    if not last:
                        stack(*at(i, q + 3))

                for u in range(3):
                    stack(*at(0, u))
                max_row(*at(0, 0))
                with sp.Fori(0, U // 2 - 2) as i:
                    for q in (0, 1):
                        step(i, q)
                step(U // 2 - 2, 0)
                step(U // 2 - 2, 1, last=True)
                step(U // 2 - 1, 0, last=True)
                load(U - 1)
                sp.wait_ge(mrow_in, 16 * U)

            @block.tensor
            def _(pe):
                def values_of(i, j):
                    w = i * 2 + j
                    pe.wait_ge(kl, w + 1)
                    pe.wait_ge(kh, w + 1)
                    row, col = w // NG * S, w % NG * P
                    for t in range(TB):
                        for n, (x, y) in enumerate(((0, 0), (0, 1), (1, 0))):
                            last = pe.matmul(k_ps[:, t * P:(t + 1) * P], L[:, x, bass.ds(row + L_CTX + t * P, P)],
                                             L[:, y, bass.ds(col + L_WKV + H, P)], start=(n == 0), stop=(n == 2))
                    last.then_inc(v_done, 1)

                def queries_of(i, j, m_of=None):
                    w_ = i * 2 + j
                    col, row = w_ % NG * P, w_ // NG * S
                    pe.wait_ge(ql, w_)
                    n = 0
                    for k in range(KC):
                        for w, x in ((0, 0), (0, 1), (1, 0)):
                            if n == 6 and m_of is not None:
                                maxima(*m_of)
                            last = pe.matmul(a_ps[:], L[:, w, bass.ds(col + L_WQ + k * H, P)], xnT[:, x, k, bass.ds(row, S)],
                                             start=(n == 0), stop=(n == 3 * KC - 1))
                            n += 1
                    last.then_inc(q_done, 1)
                    pe.wait_ge(v_copied, w_)
                    if m_of is not None:
                        pe.wait_ge(mT_copied, m_of[0] * 2 + m_of[1] + 1)
                    for n, (w, x) in enumerate(((0, 0), (0, 1), (1, 0))):
                        last = pe.matmul(k_ps[:], L[:, w, bass.ds(col + L_WKV, P)], L[:, x, bass.ds(row + L_CTX, S)],
                                         start=(n == 0), stop=(n == 2))
                    last.then_inc(k_done, 1)

                def maxima(i, j, values=1):
                    pe.wait_ge(m16_set, i * 2 + j + 1)
                    pe.wait_ge(v_copied, i * 2 + j + 1 + values)
                    pe.transpose(mT_ps, m16[:], ident[:]).then_inc(mT_done, 1)

                def stacked_rows(rows, i, j, which, h, a, b):
                    return stk[0:rows, bass.ds(slot(i, j), 1), which, h, a:b].rearrange("p a n -> p (a n)")

                def first_pass(i, j, h, ts=range(TB)):
                    u = i * 2 + j
                    if h == 0:
                        pe.wait_ge(stacked[j], (i + 1) * 16 * NST)
                    for t in ts:
                        n = u * 2 * HG + h * 2 + t // 2
                        pe.wait_ge(s_used[t % 2], n)
                        out = s_ps[t % 2]
                        pe.matmul(out[:, 0:(t + 1) * P], stacked_rows(3 * HD, i, j, 0, h, t * P, (t + 1) * P),
                                  stacked_rows(3 * HD, i, j, 1, h, 0, (t + 1) * P), start=True, stop=True)
                        pe.matmul(out[:, t * P:(t + 1) * P], bigI[:], hide[:], start=False, stop=True,
                                  skip_group_check=True).then_inc(s_done[t % 2], 1)

                def second_pass(i, j, t, hs):
                    u = i * 2 + j
                    if t == 0:
                        pe.wait_ge(mrow_in, (u + 1) * 16)
                    for h in hs:
                        pe.wait_ge(sT_used[h % 2], u * 2 * TB + t * 2 + h // 2)
                        out = sT_ps[h % 2]
                        pe.matmul(out[:, 0:S - t * P], stacked_rows(3 * HD + 1, i, j, 1, h, t * P, (t + 1) * P),
                                  stacked_rows(3 * HD + 1, i, j, 0, h, t * P, S), start=True, stop=True)
                        pe.matmul(out[:, 0:P], bigI[:], hideT[:], start=False, stop=True,
                                  skip_group_check=True).then_inc(sT_done[h % 2], 1)

                def values(i, j, t):
                    u = i * 2 + j
                    for r in range(2):
                        pe.wait_ge(sT_used[r], u * 2 * TB + (t + 1) * 2)
                    if t == 0:
                        pe.wait_ge(o_done, u)
                        pe.wait_ge(v_copied, u + 1)
                    for out, what in ((o_ps, vv), (sum_ps, None)):
                        for h in range(HG):
                            r = slice(h * HD, (h + 1) * HD)
                            lhs = ones[:] if what is None else vv[:, j, t, r]
                            last = pe.matmul(out[r, t * P:S], lhs, pT[:, t % 2, h, t * P:S], start=(t == 0),
                                             stop=(t == TB - 1), tile_position=(0, h * HD), skip_group_check=True)
                    last.then_inc(av_done[j], 1)

                def region(now, nxt=None, values_for=None):
                    for t in range(TB):
                        for half in range(2):
                            second_pass(*now, t, (2 * half, 2 * half + 1))
                            if nxt:
                                first_pass(*nxt, t, (2 * half, 2 * half + 1))
                        if t > 0:
                            values(*now, t - 1)
                    if values_for:
                        values_of(*values_for)
                    values(*now, TB - 1)

                pe.wait_ge(setup, 5)
                def step(i, q, last=False):
                    region(at(i, q), at(i, q + 1), values_for=at(i, q + 2))
                    if last:
                        maxima(*at(i, q + 1))
                    else:
                        queries_of(*at(i, q + 3), m_of=at(i, q + 1))

                queries_of(*at(0, 0))
                values_of(*at(0, 0))
                queries_of(*at(0, 1))
                values_of(*at(0, 1))
                queries_of(*at(0, 2))
                for h in range(HG):
                    first_pass(*at(0, 0), h)
                pe.wait_ge(kl, 3)
                maxima(*at(0, 0))
                pe.wait_ge(mT_copied, 1)
                pe.wait_ge(row_set, 1)
                with pe.Fori(0, U // 2 - 2) as i:
                    for q in (0, 1):
                        step(i, q)
                step(U // 2 - 2, 0)
                step(U // 2 - 2, 1, last=True)
                region(at(0, U - 2), at(0, U - 1))
                pe.wait_ge(mT_copied, U - 1)
                maxima(*at(0, U - 1), values=0)
                region(at(0, U - 1))

            @block.scalar
            def _(act):
                def queries_out(i, j):
                    u = i * 2 + j
                    act.wait_ge(q_done, u + 1)
                    act.wait_ge(stacked[j], i * 16 * NST)
                    act.activation(qk[:, j, 0], a_ps[:], ACT.Copy, scale=QS / (XS * WS)).then_inc(qh, 1)
                    act.wait_ge(k_done, u + 1)
                    act.activation(qk[:, j, 2], k_ps[:], ACT.Copy, scale=QS / (WS * WS)).then_inc(kh, 1)

                def values_out(i, j):
                    act.wait_ge(v_done, i * 2 + j + 1)
                    act.wait_ge(av_done[j], i * TB)
                    act.activation(vv[:, j].rearrange("p t n -> p (t n)"), k_ps[:], ACT.Copy, scale=1.0 / (WS * WS)).then_inc(v_copied, 1)

                def copy_max(i, j):
                    act.wait_ge(mT_done, i * 2 + j + 1)
                    act.wait_ge(mrow_in, 16 * (i * 2 + j))
                    act.activation(mT[:], mT_ps, ACT.Copy).then_inc(mT_copied, 1)

                def exps(i, j, ts):
                    u = i * 2 + j
                    for t in ts:
                        if t == 0:
                            act.wait_ge(av_done[1 - j], (i + j) * TB)
                        elif t >= 2:
                            act.wait_ge(av_done[j], i * TB + t - 1)
                        for h in range(HG):
                            act.wait_ge(sT_done[h % 2], u * 2 * TB + t * 2 + h // 2 + 1)
                            act.activation(pT[:, t % 2, h, t * P:S], sT_ps[h % 2][:, 0:S - t * P], ACT.Exp, scale=SCALE)\
                                .then_inc(sT_used[h % 2], 1)

                def output(i, j):
                    u = i * 2 + j
                    act.wait_ge(o_done, u + 1)
                    act.activation(AT[:, 0, bass.ds(u % NG, 1), bass.ds(u // NG * S, S)].rearrange("p a n -> p (a n)"),
                                   o[:], ACT.Copy, scale=AS).then_inc(ah, 1)

                def split(u):
                    act.wait_ge(w_in, 16 * u + 16)
                    act.activation(W1[:, 0, bass.ds(u * CH, CH)], stage[:], ACT.Copy, scale=WS).then_inc(w_hi, 1)

                def step(i, q, queries=True):
                    exps(*at(i, q), (0, 1))
                    output(*at(i, q - 1))
                    split(i * 2 + q - 1)
                    exps(*at(i, q), (2, 3))
                    values_out(*at(i, q + 2))
                    copy_max(*at(i, q + 1))
                    if queries:
                        queries_out(*at(i, q + 3))

                queries_out(*at(0, 0))
                values_out(*at(0, 0))
                queries_out(*at(0, 1))
                values_out(*at(0, 1))
                queries_out(*at(0, 2))
                copy_max(*at(0, 0))
                exps(*at(0, 0), range(TB))
                values_out(*at(0, 2))
                copy_max(*at(0, 1))
                queries_out(*at(0, 3))
                with act.Fori(0, U // 2 - 2) as i:
                    for q in (1, 2):
                        step(i, q)
                step(U // 2 - 2, 1, queries=False)
                exps(*at(0, U - 2), range(TB))
                copy_max(*at(0, U - 1))
                output(*at(0, U - 3))
                split(U - 3)
                exps(*at(0, U - 1), range(TB))
                for u in (U - 2, U - 1):
                    output(*at(0, u))
                    split(u)

            @block.vector
            def _(dve):
                v = nc.vector

                def project(i, j):
                    u = i * 2 + j
                    dve.wait_ge(qh, u + 1)
                    v.scalar_tensor_tensor(qk[:, j, 1], a_ps[:], QS / (XS * WS), qk[:, j, 0], ALU.mult, ALU.subtract).then_inc(ql, 1)
                    dve.wait_ge(kh, u + 1)
                    v.scalar_tensor_tensor(qk[:, j, 3], k_ps[:], QS / (WS * WS), qk[:, j, 2], ALU.mult, ALU.subtract).then_inc(kl, 1)

                def maxima(i, j, before=None):
                    u = i * 2 + j
                    for h in range(HG):
                        if h == HG - 1 and before is not None:
                            output(*before)
                            split(before[0] * 2 + before[1])
                        for t in range(TB):
                            dve.wait_ge(s_done[t % 2], u * 2 * HG + h * 2 + t // 2 + 1)
                            v.reduce_max(mx[:, j, h * TB + t:h * TB + t + 1], s_ps[t % 2][:, 0:(t + 1) * P], AX.X)\
                                .then_inc(s_used[t % 2], 1)
                    dve.wait_ge(s_used[1], (u + 1) * 2 * HG)
                    dve.wait_ge(s_used[0], (u + 1) * 2 * HG)
                    dve.wait_ge(mT_done, u)
                    v.tensor_scalar(m16[:], mx[:, j], -1.0 / WS, None, ALU.mult).then_inc(m16_set, 1)

                def average(i, j):
                    u = i * 2 + j
                    dve.wait_ge(av_done[j], (i + 1) * TB)
                    v.reciprocal(rec[:], sum_ps[:]).then_inc(rec_done, 1)
                    dve.wait_ge(rec_done, u + 1)
                    dve.wait_ge(ah, u)
                    v.tensor_tensor(o[:], o_ps[:], rec[:], ALU.mult).then_inc(o_done, 1)

                def output(i, j):
                    u = i * 2 + j
                    dve.wait_ge(ah, u + 1)
                    v.scalar_tensor_tensor(AT[:, 1, bass.ds(u % NG, 1), bass.ds(u // NG * S, S)].rearrange("p a n -> p (a n)"),
                                           o[:], AS, AT[:, 0, bass.ds(u % NG, 1), bass.ds(u // NG * S, S)].rearrange("p a n -> p (a n)"),
                                           ALU.mult, ALU.subtract).then_inc(al, 1)

                def split(u):
                    dve.wait_ge(w_hi, u + 1)
                    v.scalar_tensor_tensor(W1[:, 1, bass.ds(u * CH, CH)], stage[:], WS, W1[:, 0, bass.ds(u * CH, CH)],
                                           ALU.mult, ALU.subtract).then_inc(w_lo, 1)

                def step(i, q, queries=True):
                    maxima(*at(i, q + 1), before=at(i, q - 1))
                    average(*at(i, q))
                    if queries:
                        project(*at(i, q + 3))

                for u in range(3):
                    project(*at(0, u))
                maxima(*at(0, 0))
                maxima(*at(0, 1))
                average(*at(0, 0))
                project(*at(0, 3))
                with dve.Fori(0, U // 2 - 2) as i:
                    for q in (1, 2):
                        step(i, q)
                step(U // 2 - 2, 1, queries=False)
                maxima(*at(0, U - 1))
                output(*at(0, U - 3))
                split(U - 3)
                average(*at(0, U - 2))
                output(*at(0, U - 2))
                split(U - 2)
                average(*at(0, U - 1))
                output(*at(0, U - 1))
                split(U - 1)


def project_out(nc, d, xnT, L, W2, AT, x3, ident16):
    CH = W2_N // (NT // 2)
    with Scope(nc, "po") as s:
        xn = s.sb("xn", [P, 2, H])
        pair = s.sb("pair", [P, 2, 2 * H], F16)
        stage = s.sb("stage", [P, CH])
        mhalf = s.sb("mhalf", [P, 1])
        c = {"st": s.sb("st", [P, 2, 6]), "mv": s.sb("mv", [P, 2, 2]), "var": s.sb("var", [P, 2]), "rstd": s.sb("rstd", [P, 2])}
        o_ps = [s.ps(f"o_ps{j}", [P, H]) for j in range(2)]
        tr_ps = [s.ps(f"tr_ps{j}", [P, 2 * KC, P], F16) for j in range(2)]

        def duo(name):
            return s.sems(f"{name}0 {name}1")
        o_done, x3_done, stat, aggr, var_set, rstd_set, xn_set, hi_set, lo_set, tr_done, tr_copied = [
            duo(n) for n in "o_done x3_done stat aggr var_set rstd_set xn_set hi_set lo_set tr_done tr_copied".split()]
        x_in, mhalf_set, w_in, w_hi, w_lo = s.sems("x_in mhalf_set w_in w_hi w_lo")
        with s.block() as block:
            @block.sync
            def _(sp):
                sp.dma_start(x3[:], d["x2"]).then_inc(x_in, 16)
                with sp.Fori(0, NT // 2) as i:
                    sp.wait_ge(w_lo, i)
                    sp.dma_start(stage[:], d["w2"][:, bass.ds(i * CH, CH)]).then_inc(w_in, 16)

            @block.gpsimd
            def _(pool):
                pool.memset(mhalf[:], -0.5).then_inc(mhalf_set, 1)
                pool.wait_ge(mhalf_set, 1)
                with pool.Fori(0, NT // 2) as i:
                    for j in range(2):
                        pool.wait_ge(var_set[j], i + 1)
                        nc.gpsimd.tensor_tensor(c["rstd"][:, j:j + 1], c["var"][:, j:j + 1], mhalf[:], ALU.pow)\
                            .then_inc(rstd_set[j], 1)

            @block.tensor
            def _(pe):
                def out(i, j):
                    pe.wait_ge(x3_done[j], i)
                    n = 0
                    for g in range(NG):
                        for x, w in ((0, 0), (0, 1), (1, 0)):
                            last = pe.matmul(o_ps[j][:], AT[:, x, g, bass.ds((i * 2 + j) * P, P)],
                                             L[:, w, L_WO + g * H:L_WO + (g + 1) * H], start=(n == 0), stop=(n == 3 * NG - 1))
                            n += 1
                    last.then_inc(o_done[j], 1)

                def transposes(i, j):
                    pe.wait_ge(lo_set[j], i + 1)
                    pe.wait_ge(tr_copied[j], i)
                    for k in range(2 * KC):
                        last = pe.transpose(tr_ps[j][:, k], pair[:, j, k * P:(k + 1) * P], ident16[:])
                    last.then_inc(tr_done[j], 1)

                out(*at(0, 0))
                out(*at(0, 1))
                with pe.Fori(0, NT // 2 - 1) as i:
                    for q in (0, 1):
                        out(*at(i, q + 2))
                        transposes(*at(i, q))
                transposes(*at(0, NT - 2))
                transposes(*at(0, NT - 1))

            @block.scalar
            def _(act):
                with act.Fori(0, NT // 2) as i:
                    act.wait_ge(w_in, 16 * i + 16)
                    act.activation(W2[:, 0, bass.ds(i * CH, CH)], stage[:], ACT.Copy, scale=WS).then_inc(w_hi, 1)
                    for j in range(2):
                        act.wait_ge(xn_set[j], i + 1)
                        act.wait_ge(tr_done[j], i)
                        act.activation(pair[:, j, 0:H], xn[:, j], ACT.Copy, scale=XS).then_inc(hi_set[j], 1)
                        act.wait_ge(tr_done[j], i + 1)
                        act.activation(xnT[:, :, :, bass.ds((i * 2 + j) * P, P)].rearrange("p s k n -> p (s k) n"),
                                       tr_ps[j][:], ACT.Copy).then_inc(tr_copied[j], 1)

            @block.vector
            def _(dve):
                v = nc.vector
                dve.wait_ge(x_in, 16)
                with dve.Fori(0, NT // 2) as i:
                    for j in range(2):
                        x = x3[:, bass.ds(i * 2 + j, 1), :].rearrange("p a n -> p (a n)")
                        dve.wait_ge(o_done[j], i + 1)
                        v.scalar_tensor_tensor(x, o_ps[j][:], 1.0 / (AS * WS), x, ALU.mult, ALU.add).then_inc(x3_done[j], 1)
                        normalise_tile(nc, dve, x3_done[j], i + 1, x, j, i, c, (stat, aggr, var_set, rstd_set, xn_set, mhalf_set), xn[:, j])
                        dve.wait_ge(hi_set[j], i + 1)
                        v.scalar_tensor_tensor(pair[:, j, H:2 * H], xn[:, j], XS, pair[:, j, 0:H], ALU.mult,
                                               ALU.subtract).then_inc(lo_set[j], 1)
                    dve.wait_ge(w_hi, i + 1)
                    v.scalar_tensor_tensor(W2[:, 1, bass.ds(i * CH, CH)], stage[:], WS, W2[:, 0, bass.ds(i * CH, CH)],
                                           ALU.mult, ALU.subtract).then_inc(w_lo, 1)


GS = 16.0


def ffn1(nc, d, xnT, W1, W2, x3):
    NF = FF // P
    W1c = W1[:, :, :].rearrange("p s (k f) -> p s k f", k=KC)
    W2c = W2[:, :, :].rearrange("p s (f n) -> p s f n", f=NF)
    with Scope(nc, "ff") as s:
        hq = s.sb("hq", [P, 2, S])
        qi = s.sb("qi", [P, 2, S], I16)
        a = s.sb("a", [P, 2, S])
        aT = s.sb("aT", [P, 2, 2, S], F16)
        h_ps = [s.ps(f"h_ps{j}", [P, S]) for j in range(2)]
        y_ps = [s.ps(f"y_ps{t}", [P, H]) for t in range(TB)]

        def duo(name):
            return s.sems(f"{name}0 {name}1")
        h_done, hq_done, qi_done, a_done, hi_done, lo_done, y_used = [
            duo(n) for n in "h_done hq_done qi_done a_done hi_done lo_done y_used".split()]
        out_added, stored = s.sems("out_added stored")
        with s.block() as block:
            @block.tensor
            def _(pe):
                with pe.Fori(0, B) as b:
                    def inner(i, j):
                        pe.wait_ge(hq_done[j], b * (NF // 2) + i)
                        n = 0
                        for k in range(KC):
                            for w, x in ((0, 0), (0, 1), (1, 0)):
                                last = pe.matmul(h_ps[j][:], W1c[:, w, k, bass.ds((i * 2 + j) * P, P)],
                                                 xnT[:, x, k, bass.ds(b * S, S)], start=(n == 0), stop=(n == 3 * KC - 1))
                                n += 1
                        last.then_inc(h_done[j], 1)

                    def outer(i, j, first=False, end=False):
                        pe.wait_ge(lo_done[j], b * (NF // 2) + i + 1)
                        if first:
                            pe.wait_ge(out_added, b * TB)
                        for t in range(TB):
                            for n, (x, w) in enumerate(((0, 0), (0, 1), (1, 0))):
                                last = pe.matmul(y_ps[t][:], aT[:, j, x, t * P:(t + 1) * P],
                                                 W2c[:, w, bass.ds(i * 2 + j, 1), :].rearrange("p a n -> p (a n)"),
                                                 start=first and n == 0, stop=end and n == 2, skip_group_check=True)
                        last.then_inc(y_used[j], 1)

                    inner(*at(0, 0))
                    inner(*at(0, 1))
                    outer(*at(0, 0), first=True)
                    with pe.Fori(0, NF // 2 - 1) as i:
                        for q in (1, 2):
                            inner(*at(i, q + 1))
                            outer(*at(i, q))
                    outer(*at(0, NF - 1), end=True)

            @block.scalar
            def _(act):
                with act.Fori(0, B) as b:
                    def scaled(i, j):
                        n = b * (NF // 2) + i
                        act.wait_ge(h_done[j], n + 1)
                        act.wait_ge(qi_done[j], n)
                        act.activation(hq[:, j], h_ps[j][:], ACT.Copy, scale=10.0 / (XS * WS)).then_inc(hq_done[j], 1)

                    def gelu(i, j):
                        n = b * (NF // 2) + i
                        act.wait_ge(qi_done[j], n + 1)
                        act.wait_ge(lo_done[j], n)
                        act.activation(a[:, j], qi[:, j], ACT.Gelu_apprx_tanh, scale=0.1).then_inc(a_done[j], 1)

                    with act.Fori(0, NF // 2) as i:
                        for j in range(2):
                            scaled(i, j)
                            gelu(i, j)

            @block.vector
            def _(dve):
                v = nc.vector
                with dve.Fori(0, B) as b:
                    with dve.Fori(0, NF // 2) as i:
                        n = b * (NF // 2) + i
                        for j in range(2):
                            dve.wait_ge(hq_done[j], n + 1)
                            dve.wait_ge(a_done[j], n)
                            v.tensor_scalar(qi[:, j], hq[:, j], -32768.0, 32767.0, ALU.max, ALU.min).then_inc(qi_done[j], 1)
                            dve.wait_ge(a_done[j], n + 1)
                            dve.wait_ge(y_used[j], n)
                            v.tensor_scalar(aT[:, j, 0], a[:, j], GS, None, ALU.mult).then_inc(hi_done[j], 1)
                            dve.wait_ge(hi_done[j], n + 1)
                            v.scalar_tensor_tensor(aT[:, j, 1], a[:, j], GS, aT[:, j, 0], ALU.mult, ALU.subtract)\
                                .then_inc(lo_done[j], 1)
                    dve.wait_ge(y_used[1], (b + 1) * (NF // 2))
                    for t in range(TB):
                        x = x3[:, bass.ds(b * TB + t, 1), :].rearrange("p a n -> p (a n)")
                        v.scalar_tensor_tensor(x, y_ps[t][:], 1.0 / (GS * WS), x, ALU.mult, ALU.add).then_inc(out_added, 1)

            @block.sync
            def _(sp):
                with sp.Fori(0, B) as b:
                    sp.wait_ge(out_added, (b + 1) * TB)
                    sp.dma_start(d["out"][:, bass.ds(b * TB, TB), :], x3[:, bass.ds(b * TB, TB), :]).then_inc(stored, 16)
                sp.wait_ge(stored, 16 * B)


def build(nc, d):
    d["x1"] = nc.dram_tensor("x1_rows", [P, NT, H], F32, kind="Internal").ap()
    d["x2"] = nc.dram_tensor("x2_rows", [P, NT, H], F32, kind="Internal").ap()
    d["pairs"] = nc.dram_tensor("normalised_rows", [T, 2 * H], F16, kind="Internal").ap()
    d["ys"] = nc.dram_tensor("expert_rows", [(NT + QT) * P, H], F32, kind="Internal").ap()
    with Scope(nc, "k") as s:
        ident16 = s.sb("ident16", [P, P], F16)
        route = (s.sb("slots", [P, NT, TOPK], U32), s.sb("weights", [P, NT, TOPK]),
                 s.sb("tokens", [P, NT + QT], U32), s.sb("experts", [P, NT + QT], I32))
        (made,) = s.sems("made")
        with Scope(nc, "l0") as l0:
            logits = l0.sb("logits", [P, NT, E])
            ident = l0.sb("ident", [P, P])
            with s.block() as block:
                @block.gpsimd
                def _(pool):
                    pool.memset(ident[:], 0.0).then_inc(made, 1)
                    pool.wait_ge(made, 1)
                    pool.affine_select(out=ident[:], in_=ident[:], compare_op=ALU.not_equal, fill=1.0, base=0,
                                       pattern=[[-1, P]], channel_multiplier=1).then_inc(made, 1)
                    pool.wait_ge(made, 2)
                    nc.gpsimd.tensor_copy(ident16[:], ident[:]).then_inc(made, 1)
                    pool.wait_ge(made, 3)
            attention0(nc, d, logits, ident)
            W = l0.sb("W", [P, E + 1, EW], F16)
            routing(nc, d, W, logits, route)
            experts_ffn(nc, d, W, route, ident16)
        xnT = s.sb("xnT", [P, 2, KC, T], F16)
        W1 = s.sb("W1", [P, 2, W1_N], F16)
        with Scope(nc, "l1") as l1:
            L = l1.sb("L", [P, 2, L_N], F16)
            AT = l1.sb("AT", [P, 2, NG, T], F16)
            combine(nc, d, route, xnT, L, ident16)
            attention1(nc, d, xnT, L, W1, AT)
            with Scope(nc, "f1") as f1:
                x3 = f1.sb("x3", [P, NT, H])
                W2 = f1.sb("W2", [P, 2, W2_N], F16)
                project_out(nc, d, xnT, L, W2, AT, x3, ident16)
                ffn1(nc, d, xnT, W1, W2, x3)


def layouts(x, ctx_512, L0_xattn_W_k, L0_xattn_b_k, L0_xattn_ln_gamma, L0_xattn_ln_beta, L0_ffn_router_w,
            L0_ffn_e_bias, L0_ffn_gate_up_proj, L0_ffn_down_proj, L0_ffn_shared_gate_w, L0_ffn_shared_up_w,
            L0_ffn_shared_down_w, L1_xattn_Wq, L1_xattn_Wkv_expand, L1_xattn_Wout, L1_ffn_W1, L1_ffn_W2):
    a = np.ascontiguousarray

    def rows(w):
        return a(w.reshape(-1, P, w.shape[1]).transpose(1, 0, 2))

    def expert(gate_up, down):
        dT = down.T
        last = dT[P:EI]
        return np.concatenate([rows(gate_up.T).reshape(P, -1), dT[0:P], np.concatenate([last, last])], axis=1)

    shared_gu = np.concatenate([L0_ffn_shared_gate_w, L0_ffn_shared_up_w])
    experts = [expert(L0_ffn_gate_up_proj[e], L0_ffn_down_proj[e]) for e in range(E)]
    return {
        "x": rows(x.reshape(T, H)),
        "ctxT": a(ctx_512.reshape(T, CD).T),
        "wkT": a(L0_xattn_W_k.T), "bk": a(L0_xattn_b_k), "bk_col": a(L0_xattn_b_k.reshape(CD, 1)),
        "gamma": a(L0_xattn_ln_gamma), "beta": a(L0_xattn_ln_beta),
        "wr": rows(L0_ffn_router_w.T), "ebias": a(L0_ffn_e_bias),
        "wexp": np.stack(experts + [expert(shared_gu, L0_ffn_shared_down_w)]),
        "l1": np.concatenate([rows(L1_xattn_Wq.T).reshape(P, -1), L1_xattn_Wkv_expand.T,
                              rows(L1_xattn_Wout.T).reshape(P, -1), ctx_512.reshape(T, CD).T], axis=1),
        "w1": rows(L1_ffn_W1.T).reshape(P, -1), "w2": rows(L1_ffn_W2.T).reshape(P, -1),
    }


def kernel(**inputs):
    import concourse.bacc as bacc
    from concourse.bass_utils import run_bass_kernel_spmd

    nc = bacc.Bacc("TRN2", target_bir_lowering=False, num_devices=1)
    arrays = layouts(**{name: np.asarray(a) for name, a in inputs.items()})
    d = {name: nc.dram_tensor(f"in_{name}", a.shape, mybir.dt.from_np(a.dtype), kind="ExternalInput").ap()
         for name, a in arrays.items()}
    d["out"] = nc.dram_tensor("out_rows", (P, NT, H), F32, kind="ExternalOutput").ap()
    build(nc, d)
    got = run_bass_kernel_spmd(nc, [{f"in_{name}": a for name, a in arrays.items()}], core_ids=[0]).results[0]["out_rows"]
    return np.ascontiguousarray(got.transpose(1, 0, 2)).reshape(B, S, H)
```
